# Optimizing a Trainium2 kernel written in Bass

```python
import numpy as np
import jax
import jax.numpy as jnp

def _softmax(x, axis=-1):
    return jax.nn.softmax(x, axis=axis)

def _gelu(x):
    return jax.nn.gelu(x, approximate=True)

def _silu(x):
    return jax.nn.silu(x)

def _sigmoid(x):
    return jax.nn.sigmoid(x)

def _layernorm(x, axis=-1, eps=1e-05):
    m = jnp.mean(x, axis=axis, keepdims=True)
    v = jnp.var(x, axis=axis, keepdims=True)
    return (x - m) / jnp.sqrt(v + eps)

def _scatter_add(tgt, idx, src, axis=0):
    return tgt.at[idx].add(src)

def _segment_sum(src, seg, n):
    return jax.ops.segment_sum(src, seg, n)
kernel_name = 'mk_gnn_resnorm_d4_gnn_r32_fb7b30'

def setup_inputs(seed: int=0):
    np.random.seed(seed)
    _w = jnp.asarray

    def _rec_inputs():
        import jax
        import jax.numpy as jnp
        _gk = jax.random.key(seed)
        x = -0.000202 + 1 * jax.random.normal(jax.random.fold_in(_gk, 1), (3125, 128), jnp.float32)
        _s = jax.random.randint(jax.random.fold_in(_gk, 2), (50000,), 0, 3125, jnp.int32)
        _d = jax.random.randint(jax.random.fold_in(_gk, 3), (50000,), 0, 3125, jnp.int32)
        _loop = jnp.arange(3125, dtype=jnp.int32)
        src = jnp.concatenate([_s, _d, _loop])
        dst = jnp.concatenate([_d, _s, _loop])
        _o = jnp.argsort(dst, stable=True)
        src = src[_o]
        dst = dst[_o]
        edge_attr_6 = 0.00011001 + 1.00018 * jax.random.normal(jax.random.fold_in(_gk, 12), (103125, 6), jnp.float32)
        edge_weight = jax.random.uniform(jax.random.fold_in(_gk, 15), (103125,), jnp.float32, 0.0, 0.999998)
        return (x, src, dst, edge_attr_6, edge_weight)
    x, src, dst, edge_attr_6, edge_weight = _rec_inputs()

    def _L0_gnn_setup():
        import jax, jax.numpy as jnp
        import numpy as np
        N_NODES = 50000
        N_EDGES = 25000
        D_IN = 128
        D_OUT = 128
        key = jax.random.key(seed)
        ks = jax.random.split(key, 8)
        x = jax.random.normal(ks[0], (N_NODES, D_IN), dtype=jnp.float32)
        edge_index = jax.random.randint(ks[1], (2, N_EDGES), 0, N_NODES, dtype=jnp.int64)
        s = 1.0 / np.sqrt(D_IN)
        so = 1.0 / np.sqrt(D_OUT)
        W1 = jax.random.uniform(ks[2], (D_IN, D_OUT), jnp.float32, -s, s)
        b1 = jax.random.uniform(ks[3], (D_OUT,), jnp.float32, -s, s)
        W2 = jax.random.uniform(ks[4], (D_OUT, D_OUT), jnp.float32, -so, so)
        b2 = jax.random.uniform(ks[5], (D_OUT,), jnp.float32, -so, so)
        Wres = jax.random.uniform(ks[6], (D_IN, D_OUT), jnp.float32, -s, s)
        bres = jax.random.uniform(ks[7], (D_OUT,), jnp.float32, -s, s)
        return {'x': x, 'edge_index': edge_index, 'W1': W1, 'b1': b1, 'W2': W2, 'b2': b2, 'Wres': Wres, 'bres': bres}
    _L0_gnn_all = _L0_gnn_setup()
    _L0_gnn_in = {k: v for k, v in _L0_gnn_all.items() if k in ('W1', 'b1', 'W2', 'b2', 'Wres', 'bres')}
    del _L0_gnn_all

    def _L1_gnn_setup():
        import jax, jax.numpy as jnp
        import numpy as np
        N_NODES = 3125
        N_EDGES = 50000
        D = 128

        def mean_agg(x, src, dst, n):
            s = jax.ops.segment_sum(x[src], dst, num_segments=n)
            deg = jax.ops.segment_sum(jnp.ones(src.shape[0], x.dtype), dst, num_segments=n)
            return s / jnp.maximum(deg, 1.0)[:, None]

        def gin_layer(x, Wa, ba, Wb, bb):
            h = x @ Wa.T + ba
            h = h @ Wb.T + bb
            return jax.nn.relu(h)
        key = jax.random.key(seed)
        ks = jax.random.split(key, 8)
        sc = 1.0 / np.sqrt(D)
        return {'features': jax.random.normal(ks[0], (N_NODES, D), jnp.float32), 'src': jax.random.randint(ks[1], (N_EDGES,), 0, N_NODES, jnp.int32), 'dst': jax.random.randint(ks[2], (N_EDGES,), 0, N_NODES, jnp.int32), 'W1a': jax.random.normal(ks[3], (D, D), jnp.float32) * sc, 'b1a': jnp.zeros((D,), jnp.float32), 'W1b': jax.random.normal(ks[4], (D, D), jnp.float32) * sc, 'b1b': jnp.zeros((D,), jnp.float32), 'W2a': jax.random.normal(ks[5], (D, D), jnp.float32) * sc, 'b2a': jnp.zeros((D,), jnp.float32), 'W2b': jax.random.normal(ks[6], (D, D), jnp.float32) * sc, 'b2b': jnp.zeros((D,), jnp.float32)}
    _L1_gnn_all = _L1_gnn_setup()
    _L1_gnn_in = {k: v for k, v in _L1_gnn_all.items() if k in ('W1a', 'b1a', 'W1b', 'b1b', 'W2a', 'b2a', 'W2b', 'b2b')}
    del _L1_gnn_all

    def _L2_gnn_setup():
        import jax, jax.numpy as jnp
        import numpy as np
        N, D, E = (50000, 128, 25000)
        NUM_ITERS = 4
        EPS = 0.1
        GAMMA = 0.1
        key = jax.random.key(seed)
        k1, k2, k3, k4, k5, k6 = jax.random.split(key, 6)
        x = jax.random.normal(k1, (N, D), dtype=jnp.float32)
        edge_index = jax.random.randint(k2, (2, E), 0, N, dtype=jnp.int64)
        edge_weight = jax.random.uniform(k3, (E,), dtype=jnp.float32)
        W = jax.random.normal(k4, (D, D), dtype=jnp.float32) * 0.05
        bias = jax.random.normal(k5, (D,), dtype=jnp.float32) * 0.05
        W_phi = jax.random.normal(k6, (D, D), dtype=jnp.float32) * 0.05
        return {'x': x, 'edge_index': edge_index, 'edge_weight': edge_weight, 'W': W, 'bias': bias, 'W_phi': W_phi}
    _L2_gnn_all = _L2_gnn_setup()
    _L2_gnn_in = {k: v for k, v in _L2_gnn_all.items() if k in ('W', 'bias', 'W_phi')}
    del _L2_gnn_all

    def _L3_gnn_setup():
        import jax, jax.numpy as jnp
        import numpy as np
        N_NODES = 50000
        N_EDGES = 25000
        IN_F = 128
        OUT_F = 128
        EDGE_F = 6
        key = jax.random.key(seed)
        k1, k2, k3, k4, k5, k6, k7 = jax.random.split(key, 7)
        nodeFeatures = jax.random.normal(k1, (N_NODES, IN_F), dtype=jnp.float32)
        edgeIndex = jax.random.randint(k2, (N_EDGES, 2), 0, N_NODES, dtype=jnp.int64)
        edgeFeatures = jax.random.normal(k3, (N_EDGES, EDGE_F), dtype=jnp.float32)
        lim_n = 1.0 / np.sqrt(IN_F)
        lim_e = 1.0 / np.sqrt(EDGE_F)
        W = jax.random.uniform(k4, (IN_F, OUT_F), minval=-lim_n, maxval=lim_n, dtype=jnp.float32)
        b = jax.random.uniform(k5, (OUT_F,), minval=-lim_n, maxval=lim_n, dtype=jnp.float32)
        We = jax.random.uniform(k6, (EDGE_F, OUT_F), minval=-lim_e, maxval=lim_e, dtype=jnp.float32)
        be = jax.random.uniform(k7, (OUT_F,), minval=-lim_e, maxval=lim_e, dtype=jnp.float32)
        return {'nodeFeatures': nodeFeatures, 'edgeIndex': edgeIndex, 'edgeFeatures': edgeFeatures, 'W': W, 'b': b, 'We': We, 'be': be}
    _L3_gnn_all = _L3_gnn_setup()
    _L3_gnn_in = {k: v for k, v in _L3_gnn_all.items() if k in ('W', 'b', 'We', 'be')}
    del _L3_gnn_all
    return {'x': x, 'src': src, 'dst': dst, 'edge_attr_6': edge_attr_6, 'edge_weight': edge_weight, 'L0_gnn_W1': _L0_gnn_in['W1'], 'L0_gnn_b1': _L0_gnn_in['b1'], 'L0_gnn_W2': _L0_gnn_in['W2'], 'L0_gnn_b2': _L0_gnn_in['b2'], 'L0_gnn_Wres': _L0_gnn_in['Wres'], 'L0_gnn_bres': _L0_gnn_in['bres'], 'L1_gnn_W1a': _L1_gnn_in['W1a'], 'L1_gnn_b1a': _L1_gnn_in['b1a'], 'L1_gnn_W1b': _L1_gnn_in['W1b'], 'L1_gnn_b1b': _L1_gnn_in['b1b'], 'L1_gnn_W2a': _L1_gnn_in['W2a'], 'L1_gnn_b2a': _L1_gnn_in['b2a'], 'L1_gnn_W2b': _L1_gnn_in['W2b'], 'L1_gnn_b2b': _L1_gnn_in['b2b'], 'L2_gnn_W': _L2_gnn_in['W'], 'L2_gnn_bias': _L2_gnn_in['bias'], 'L2_gnn_W_phi': _L2_gnn_in['W_phi'], 'L3_gnn_W': _L3_gnn_in['W'], 'L3_gnn_b': _L3_gnn_in['b'], 'L3_gnn_We': _L3_gnn_in['We'], 'L3_gnn_be': _L3_gnn_in['be']}

def reference(x, src, dst, edge_attr_6, edge_weight, L0_gnn_W1, L0_gnn_b1, L0_gnn_W2, L0_gnn_b2, L0_gnn_Wres, L0_gnn_bres, L1_gnn_W1a, L1_gnn_b1a, L1_gnn_W1b, L1_gnn_b1b, L1_gnn_W2a, L1_gnn_b2a, L1_gnn_W2b, L1_gnn_b2b, L2_gnn_W, L2_gnn_bias, L2_gnn_W_phi, L3_gnn_W, L3_gnn_b, L3_gnn_We, L3_gnn_be):
    import jax
    import jax.numpy as jnp

    def _L0_gnn_ref(x, edge_index, W1, b1, W2, b2, Wres, bres):
        import jax, jax.numpy as jnp
        import numpy as np
        N_NODES = 50000
        N_EDGES = 25000
        D_IN = 128
        D_OUT = 128
        src = edge_index[0]
        dst = edge_index[1]
        agg = jax.ops.segment_sum(x[src], dst, num_segments=x.shape[0])
        h = x + agg
        h = jnp.maximum(h @ W1 + b1, 0.0) @ W2 + b2
        res = x @ Wres + bres
        return res + h

    def _L1_gnn_ref(features, src, dst, W1a, b1a, W1b, b1b, W2a, b2a, W2b, b2b):
        import jax, jax.numpy as jnp
        import numpy as np
        N_NODES = 3125
        N_EDGES = 50000
        D = 128

        def mean_agg(x, src, dst, n):
            s = jax.ops.segment_sum(x[src], dst, num_segments=n)
            deg = jax.ops.segment_sum(jnp.ones(src.shape[0], x.dtype), dst, num_segments=n)
            return s / jnp.maximum(deg, 1.0)[:, None]

        def gin_layer(x, Wa, ba, Wb, bb):
            h = x @ Wa.T + ba
            h = h @ Wb.T + bb
            return jax.nn.relu(h)
        n = features.shape[0]
        h = features + mean_agg(features, src, dst, n)
        h = gin_layer(h, W1a, b1a, W1b, b1b)
        h = jax.nn.relu(h)
        h2 = h + mean_agg(h, src, dst, n)
        out = gin_layer(h2, W2a, b2a, W2b, b2b)
        return out

    def _L2_gnn_ref(x, edge_index, edge_weight, W, bias, W_phi):
        import jax, jax.numpy as jnp
        import numpy as np
        N, D, E = (50000, 128, 25000)
        NUM_ITERS = 4
        EPS = 0.1
        GAMMA = 0.1
        n, d = x.shape
        src, dst = (edge_index[0], edge_index[1])
        A = W - W.T - GAMMA * jnp.eye(d, dtype=W.dtype)
        deg = jnp.zeros((n,), dtype=x.dtype).at[dst].add(edge_weight) + 1.0
        dinv = jax.lax.rsqrt(deg)
        norm = dinv[src] * dinv[dst] * edge_weight
        self_norm = dinv * dinv

        def step(xc, _):
            h = xc @ W_phi.T
            neigh = jnp.zeros_like(h).at[dst].add(norm[:, None] * h[src])
            neigh = neigh + self_norm[:, None] * h
            conv = xc @ A.T + neigh + bias
            return (xc + EPS * jnp.tanh(conv), None)
        out, _ = jax.lax.scan(step, x, None, length=NUM_ITERS)
        return out

    def _L3_gnn_ref(nodeFeatures, edgeIndex, edgeFeatures, W, b, We, be):
        import jax, jax.numpy as jnp
        import numpy as np
        N_NODES = 50000
        N_EDGES = 25000
        IN_F = 128
        OUT_F = 128
        EDGE_F = 6
        transformed = nodeFeatures @ W + b
        edgeMsg = edgeFeatures @ We + be
        src = edgeIndex[:, 0]
        dst = edgeIndex[:, 1]
        messages = transformed[src] + edgeMsg
        aggregated = jax.ops.segment_sum(messages, dst, num_segments=nodeFeatures.shape[0])
        return jax.nn.relu(aggregated)
    edge_index = jnp.stack([src, dst])
    edge_index_t = jnp.stack([src, dst], axis=1)
    x = _layernorm(x + _L0_gnn_ref(x, edge_index, L0_gnn_W1, L0_gnn_b1, L0_gnn_W2, L0_gnn_b2, L0_gnn_Wres, L0_gnn_bres), axis=-1)
    x = _layernorm(x + _L1_gnn_ref(x, src, dst, L1_gnn_W1a, L1_gnn_b1a, L1_gnn_W1b, L1_gnn_b1b, L1_gnn_W2a, L1_gnn_b2a, L1_gnn_W2b, L1_gnn_b2b), axis=-1)
    x = _layernorm(x + _L2_gnn_ref(x, edge_index, edge_weight, L2_gnn_W, L2_gnn_bias, L2_gnn_W_phi), axis=-1)
    x = _layernorm(x + _L3_gnn_ref(x, edge_index_t, edge_attr_6, L3_gnn_W, L3_gnn_b, L3_gnn_We, L3_gnn_be), axis=-1)
    return x

_drawn_inputs = setup_inputs


def setup_inputs(seed=0):
    import zlib

    import numpy as np

    out = dict(_drawn_inputs(seed))
    spreads = {'L1_gnn_b1a': (0.0, 0.1),
     'L1_gnn_b1b': (0.0, 0.1),
     'L1_gnn_b2a': (0.0, 0.1),
     'L1_gnn_b2b': (0.0, 0.1)}
    factors = {'edge_weight': 8.0, 'L0_gnn_b1': 4.302, 'L2_gnn_bias': 6.26}
    for name, (base, spread) in spreads.items():
        noise = np.random.default_rng([zlib.crc32(name.encode()), seed]).standard_normal(out[name].shape)
        drawn = base * np.exp(spread * noise) if base else spread * noise
        out[name] = jnp.asarray(drawn.astype(out[name].dtype))
    for name, factor in factors.items():
        out[name] = (out[name] * factor).astype(out[name].dtype)
    return out
```

```python
from contextlib import ExitStack

import concourse.bass as bass
from concourse import mybir

F32 = mybir.dt.float32
F16 = mybir.dt.float16
BF16 = mybir.dt.bfloat16
I32 = mybir.dt.int32
ALU = mybir.AluOpType
ACT = mybir.ActivationFunctionType
AX = mybir.AxisListType.X

NODES = 3125
EDGES = 103125
D = 128
NP = 125
NC = NODES // NP
SLOTS = 64
PAIRS = (NC + 1) // 2
BLOCK = 256
NBLK = -(-(EDGES + SLOTS) // BLOCK)
EP = NBLK * BLOCK
FE = 8
TS = 25
STEPS = NP // TS
BT = 5
GRP = 4
GROUPS = -(-NC // GRP)
GCOL = GRP * NP
KCH = 5
ROUNDS = 8
EPS_LN = 1e-5
GAMMA = 0.1
EPS_STEP = 0.1
ROUND_MAGIC = 1.5 * 2 ** 23


def chunks_of(g):
    return min(GRP, NC - GRP * g)


def layer_of(r):
    return [0, 1, 1, 2, 2, 2, 2, 3][r]


def build_program(nc, x, edge_pairs, dst_blocks, edge_feats, w, out):
    ctx = ExitStack()
    with ctx:
        def sb(name, shape, dt=F32):
            return ctx.enter_context(nc.sbuf_tensor(name, shape, dt))

        def sem(name):
            return ctx.enter_context(nc.semaphore(name))

        mats = nc.dram_tensor("mats", (3, PAIRS, NP, NC * 2 * NP), F16).ap()

        ps = ctx.enter_context(nc.psum_tensor("ps", [128, 8, 512], F32))

        ident = sb("ident", [128, 128])
        Xn = sb("Xn", [NP, NC, D])
        XT = sb("XT", [D, NODES])
        parts_even = sb("parts_even", [NP, 3, NC, D], BF16)
        S8 = sb("S8", [NP, NC, FE])
        dinv = sb("dinv", [NP, NC])
        degr = sb("degr", [NP, NC])
        dval = sb("dval", [NP, NC + 1])
        eps_col = sb("eps_col", [128, 1])
        one_col = sb("one_col", [128, 1])
        sel0 = sb("sel0", [FE, 128])
        Wn = {k: sb("sb_" + k, [D, D]) for k in ("L0_W1", "L0_W2", "L0_Wres", "L3_W")}
        WT = {k: sb("sbT_" + k, [D, D]) for k in ("L1_W1a", "L1_W1b", "L1_W2a", "L1_W2b", "L2_W", "L2_Wphi")}
        W8 = sb("W8", [FE, D])
        be_row = sb("be_row", [1, D])
        bcol = sb("bcol", [D, 3])
        brow = sb("brow", [NP, 5, D])
        stats = sb("stats", [NP, 2, GRP, 6])
        mv = sb("mv", [NP, 2, GRP, 2])
        std = sb("std", [NP, 2, GRP])
        rstd = sb("rstd", [NP, 2, GRP])
        ones_row = sb("ones_row", [1, NP])
        ptrf = sb("ptrf", [NP, NC])
        blkf = sb("blkf", [NP, NC])
        blki = sb("blki", [NP, NC], I32)
        ptr2 = sb("ptr2", [NP, NC], I32)
        ptr8 = sb("ptr8", [NP, NC], I32)

        ARENA = 155776
        arena = sb("arena", [128, ARENA // 4])

        def at(off, parts, shape, dt=F32):
            size = 4 if dt in (F32, I32) else 2
            n = 1
            for s in shape:
                n *= s
            assert off % 4 == 0 and off + n * size <= ARENA, (off, shape)
            v = arena[0:parts, off // 4:off // 4 + -(-n * size // 4)]
            if dt != F32:
                v = v.bitcast(dt)[:, 0:n]
            names = "abcde"[:len(shape)]
            if len(shape) > 1:
                v = v.rearrange(f"p ({' '.join(names)}) -> p {' '.join(names)}",
                                **{names[i]: shape[i] for i in range(1, len(shape))})
            return v

        first_rep = at(75000, NP, [NBLK])
        blk_first = at(80000, 1, [NBLK], I32)
        blk_firstf = at(84000, 1, [NBLK])
        cmp1 = at(0, NP, [NC, NBLK])
        dblk = at(0, NP, [NC, BLOCK], I32)
        cmp2 = at(25600, NP, [NC, BLOCK])
        fe = at(0, NP, [NC, SLOTS, FE])
        sd = at(51200, NP, [NC, SLOTS, 2], I32)
        tmpR = at(64000, NP, [NC + 1, SLOTS])
        rec = [at(75000 + 6656 * i, NP, [NC + 1, SLOTS]) for i in range(5)]
        hiR, loR, cntR, w1R, w2R = rec
        w1h = at(70656, NP, [NC + 1, SLOTS], F16)
        raw_w = at(108280, D, [6, D])
        stg = at(0, NP, [2, 3, 2 * NC, NP], F16)
        hot_hi = [at(75000 + 13752 * i, 128, [NP, TS], F16) for i in range(3)]
        hot_lo = [at(75000 + 13752 * i + 6252, 128, [3, NC, 2, TS], F16) for i in range(3)]
        iota_hi = at(116256, 128, [NP, TS], F16)
        iota_lo = at(122508, 128, [NC, TS], F16)
        eq_lo = [at(123760 + 1252 * i, 128, [NC, TS], F16) for i in range(3)]
        hi_c = at(127516, 128, [PAIRS + 1, NP], F16)
        lo_c = at(131016, 128, [PAIRS + 1, NP], F16)
        val_c = at(134516, 128, [3, 2, PAIRS + 1, NP], F16)
        RING = 4
        ring = [at(25000 * i, NP, [2, NC, 2 * NP], F16) for i in range(RING)]
        T1 = [at(100000 + 2000 * i, D, [GCOL]) for i in range(2)]
        T2 = [at(104000 + 2000 * i, D, [GCOL]) for i in range(2)]
        Y = [at(108000 + 2048 * i, NP, [GRP, D]) for i in range(2)]
        Z = [at(112096 + 2048 * i, NP, [GRP, D]) for i in range(2)]
        parts_odd = at(116192, NP, [2, NC, D], F16)
        Cn = at(128992, NP, [GROUPS * GRP, D])
        inv_deg = at(128992, D, [GROUPS, GRP * D])
        S8T = [at(143328 + 2000 * i, FE, [GCOL]) for i in range(2)]

        def parts(r):
            if r % 2:
                return parts_odd
            return parts_even if r < 3 else parts_even[:, :, :, :].bitcast(F16)

        def n_parts(r):
            return 3 if r in (0, 2) else 2

        consts = sem("consts")
        x_in = sem("x_in")
        first_in = sem("first_in")
        w_in = sem("w_in")
        firstf_ok = sem("firstf_ok")
        first_ps = sem("first_ps")
        blk_ok = sem("blk_ok")
        dblk_in = sem("dblk_in")
        ptr_ok = sem("ptr_ok")
        sd_in = sem("sd_in")
        fe_in = sem("fe_in")
        rec_ok = sem("rec_ok")
        col_ps = sem("col_ps")
        col_ok = sem("col_ok")
        wt_ps = sem("wt_ps")
        wt_ok = sem("wt_ok")
        deg_ok = sem("deg_ok")
        sq_ok = sem("sq_ok")
        xt_ps = sem("xt_ps")
        xt0_ok = sem("xt0_ok")
        parts0_ok = sem("parts0_ok")
        iotas = sem("iotas")
        cols_zero = sem("cols_zero")
        dve_chain = sem("dve_chain")
        eq_ok = sem("eq_ok")
        hots_ok = sem("hots_ok")
        unit_mm = sem("unit_mm")
        unit_act = sem("unit_act")
        unit_free = sem("unit_free")
        stg_free = sem("stg_free")
        mats_out = sem("mats_out")
        s8t_ps0 = sem("s8t_ps0")
        s8t_ok0 = sem("s8t_ok0")
        rep_ps = sem("rep_ps")
        rep_ok = sem("rep_ok")
        slot_in = [sem(f"slot_in{i}") for i in range(RING)]
        item_used = sem("item_used")
        t1_ready = sem("t1_ready")
        s1_done = sem("s1_done")
        t2_ready = sem("t2_ready")
        s2_done = sem("s2_done")
        s2_read = sem("s2_read")
        pre_tanh = sem("pre_tanh")
        tanh_ok = sem("tanh_ok")
        var_ready = sem("var_ready")
        std_ready = sem("std_ready")
        v_ready = sem("v_ready")
        parts_ready = sem("parts_ready")
        s3_done = sem("s3_done")
        xt_ready = sem("xt_ready")
        y_ready = sem("y_ready")
        y_out = [sem(f"y_out{i}") for i in range(2)]

        items = [(r, g, m) for r in range(ROUNDS) for g in range(GROUPS)
                 for m in ((1, 2) if layer_of(r) == 2 else (0,))]
        item_no = {it: i for i, it in enumerate(items)}
        BUILD = PAIRS * STEPS

        block = ctx.enter_context(nc.Block())

        @block.sync
        def _(sp):
            sp.dma_start(blk_first, dst_blocks[:, 0:1].rearrange("b o -> o b"),
                         allow_slow_non_contiguous=True).then_inc(first_in, 16)
            sp.dma_start(Xn[:, :, :], x.rearrange("(p c) f -> p c f", c=NC)).then_inc(x_in, 16)
            for k, t in Wn.items():
                sp.dma_start(t[:, :], w[k]).then_inc(w_in, 16)
            for i, k in enumerate(WT):
                sp.dma_start(raw_w[:, i, :], w[k]).then_inc(w_in, 16)
            for i, k in enumerate(("L0_b1", "L1_b1a", "L1_b2a")):
                sp.dma_start(bcol[:, i:i + 1], w[k].rearrange("(d o) -> d o", o=1),
                             allow_slow_non_contiguous=True).then_inc(w_in, 16)
            for i, k in enumerate(("L0_b2", "L0_bres", "L1_b1b", "L1_b2b", "L2_bias")):
                sp.dma_start(brow[:, i, :], w[k].rearrange("(o d) -> o d", o=1).to_broadcast([NP, D])).then_inc(w_in, 16)
            sp.wait_ge(consts, 2)
            sp.dma_start(W8[0:1, :], w["L3_b"].rearrange("(o d) -> o d", o=1)).then_inc(w_in, 16)
            sp.dma_start(W8[2:FE, :], w["L3_We"]).then_inc(w_in, 16)
            sp.dma_start(be_row[:, :], w["L3_be"].rearrange("(o d) -> o d", o=1)).then_inc(w_in, 16)

            sp.sem_inc(stg_free, 2)
            with sp.Fori(0, PAIRS) as q:
                sp.wait_ge(unit_free, 2 * STEPS * q + 2 * STEPS + 2)
                for m in range(3):
                    sp.dma_start(mats[m, bass.ds(q, 1)].rearrange("a p n -> (a p) n"),
                                 stg[:, bass.ds(q % 2, 1), m].rearrange("p a j n -> p (a j n)")).then_inc(mats_out, 16)
                sp.wait_ge(mats_out, 48 * q + 48)
                sp.sem_inc(stg_free, 1)

            def store_out(g):
                q = GROUPS * (ROUNDS - 1) + g
                sp.wait_ge(y_ready, g + 1)
                n = chunks_of(g)
                sp.dma_start(out.rearrange("(p c) f -> p c f", c=NC)[:, GRP * g:GRP * g + n, :],
                             Z[q % 2][:, 0:n, :]).then_inc(y_out[g % 2], 16)

            sp.wait_ge(rep_ok, GROUPS)
            for i, (r, g, m) in enumerate(items):
                if i >= RING:
                    sp.wait_ge(item_used, i - RING + 1)
                n = 2 if g < GROUPS - 1 else 1
                sp.dma_start(ring[i % RING][:, 0:n, :, :].rearrange("p q k n -> p q (k n)"),
                             mats[m, 2 * g:2 * g + n].rearrange("q p n -> p q n")).then_inc(slot_in[i % RING], 16)
            for g in range(GROUPS):
                store_out(g)
            sp.wait_ge(y_out[0], 16 * ((GROUPS + 1) // 2))
            sp.wait_ge(y_out[1], 16 * (GROUPS // 2))

        @block.gpsimd
        def _(pool):
            nc.gpsimd.memset(ident[:, :], 0.0)
            nc.gpsimd.memset(eps_col[:, :], EPS_LN)
            nc.gpsimd.memset(one_col[:, :], 1.0)
            nc.gpsimd.memset(ones_row[:, :], 1.0)
            nc.gpsimd.memset(sel0[:, :], 0.0)
            nc.gpsimd.iota(dval[:, :], [[1, NC + 1]], base=0, channel_multiplier=NC,
                           allow_small_or_imprecise_dtypes=True)
            nc.gpsimd.memset(W8[:, :], 0.0).then_inc(consts, 1)
            pool.wait_ge(consts, 1)
            nc.gpsimd.memset(sel0[0:1, :], 1.0)
            nc.gpsimd.affine_select(out=ident[:, :], in_=ident[:, :], compare_op=ALU.not_equal, fill=1.0,
                                    base=0, pattern=[[-1, 128]], channel_multiplier=1).then_inc(consts, 1)
            nc.gpsimd.iota(iota_hi, [[1, NP], [0, TS]], base=0, channel_multiplier=0,
                           allow_small_or_imprecise_dtypes=True)
            nc.gpsimd.iota(iota_lo, [[1, NC], [0, TS]], base=0, channel_multiplier=0,
                           allow_small_or_imprecise_dtypes=True).then_inc(iotas, 1)
            nc.gpsimd.memset(hi_c, 0.0)
            nc.gpsimd.memset(lo_c, 0.0)
            nc.gpsimd.memset(val_c, 0.0).then_inc(cols_zero, 1)

            pool.wait_ge(blk_ok, 1)
            for c in range(NC):
                nc.gpsimd.indirect_dma_start(dblk[:, c, :], None, dst_blocks,
                                             bass.IndirectOffsetOnAxis(blki[:, c:c + 1], 0)).then_inc(dblk_in, 16)
            pool.wait_ge(ptr_ok, 1)
            pairs_v = edge_pairs.rearrange("(a b) t -> a (b t)", b=SLOTS)
            feats_v = edge_feats.rearrange("(a b) t -> a (b t)", b=SLOTS)
            for c in range(NC):
                nc.gpsimd.indirect_dma_start(sd[:, c].rearrange("p s t -> p (s t)"), None, pairs_v,
                                             bass.IndirectOffsetOnAxis(ptr2[:, c:c + 1], 1)).then_inc(sd_in, 16)
            for c in range(NC):
                nc.gpsimd.indirect_dma_start(fe[:, c].rearrange("p s t -> p (s t)"), None, feats_v,
                                             bass.IndirectOffsetOnAxis(ptr8[:, c:c + 1], 1)).then_inc(fe_in, 16)

        @block.vector
        def _(dve):
            v = nc.vector
            chain = [0]

            def link(ins):
                ins.then_inc(dve_chain, 1)
                chain[0] += 1
                dve.wait_ge(dve_chain, chain[0])

            dve.wait_ge(first_in, 16)
            v.tensor_copy(blk_firstf, blk_first).then_inc(firstf_ok, 1)
            dve.wait_ge(first_ps, 1)
            dve.wait_ge(consts, 2)
            link(v.tensor_copy(first_rep, ps[0:NP, 0, 0:NBLK]))
            d_c = dval[:, 0:NC].unsqueeze(2)
            link(v.tensor_tensor(cmp1, first_rep.unsqueeze(1).to_broadcast([NP, NC, NBLK]),
                                 d_c.to_broadcast([NP, NC, NBLK]), ALU.is_lt))
            link(v.tensor_reduce(blkf[:, :], cmp1, AX, ALU.add))
            link(v.tensor_scalar(blkf[:, :], blkf[:, :], -1.0, 0.0, ALU.add, ALU.max))
            v.tensor_copy(blki[:, :], blkf[:, :]).then_inc(blk_ok, 1)

            dve.wait_ge(x_in, 16)
            link(v.tensor_copy(parts_even[:, 0], Xn[:, :, :]))
            rest = at(51200, NP, [NC, D])
            link(v.tensor_tensor(rest, Xn[:, :, :], parts_even[:, 0], ALU.subtract))
            link(v.tensor_copy(parts_even[:, 1], rest))
            v.tensor_tensor(parts_even[:, 2], rest, parts_even[:, 1], ALU.subtract).then_inc(parts0_ok, 1)
            dve.wait_ge(parts0_ok, 1)

            dve.wait_ge(dblk_in, 16 * NC)
            link(v.tensor_tensor(cmp2, dblk, d_c.to_broadcast([NP, NC, BLOCK]), ALU.is_lt))
            link(v.tensor_reduce(ptrf[:, :], cmp2, AX, ALU.add))
            link(v.scalar_tensor_tensor(ptrf[:, :], blkf[:, :], float(BLOCK), ptrf[:, :], ALU.mult, ALU.add))
            v.tensor_scalar(ptr2[:, :], ptrf[:, :], 2.0, None, ALU.mult)
            v.tensor_scalar(ptr8[:, :], ptrf[:, :], float(FE), None, ALU.mult).then_inc(ptr_ok, 1)

            dve.wait_ge(sd_in, 16 * NC)
            last = SLOTS - 1
            link(v.memset(rec[2], 0.0))
            link(v.memset(rec[3], 0.0))
            link(v.memset(rec[0], 0.0))
            link(v.tensor_tensor(cntR[:, 0:NC, :], sd[:, :, :, 1], d_c.to_broadcast([NP, NC, SLOTS]), ALU.is_equal))
            link(v.tensor_copy(hiR[:, 0:NC, :], sd[:, :, :, 0]))
            link(v.tensor_copy(hiR[:, 0:NC, last], dval[:, 0:NC]))
            link(v.memset(cntR[:, :, last], 0.0))
            link(v.tensor_scalar(tmpR, hiR, 1.0 / NC, -0.5 + 0.5 / NC, ALU.mult, ALU.add))
            link(v.tensor_scalar(tmpR, tmpR, ROUND_MAGIC, -ROUND_MAGIC, ALU.add, ALU.add))
            link(v.scalar_tensor_tensor(loR, tmpR, -float(NC), hiR, ALU.mult, ALU.add))
            v.tensor_copy(hiR, tmpR).then_inc(rec_ok, 1)
            dve.wait_ge(fe_in, 16 * NC)
            dve.wait_ge(rec_ok, 1)
            link(v.tensor_tensor(w1R[:, 0:NC, :], fe[:, :, :, 1], cntR[:, 0:NC, :], ALU.mult))
            link(v.memset(w1R[:, 0:NC, last], 1.0))
            link(v.tensor_copy(w1h, w1R))
            link(v.tensor_tensor(w2R, w1R, w1h, ALU.subtract))
            v.tensor_copy(w1R, w1h).then_inc(rec_ok, 1)

            def cols_out(b):
                k, g = divmod(b, 4)
                n = min(4, PAIRS - 4 * g)
                dve.wait_ge(col_ps, b + 1)
                src = ps[:, b % 4, 0:n * NP].rearrange("p (q t) -> p q t", t=NP)
                if k < 2:
                    dst = (hi_c, lo_c)[k]
                    return v.tensor_copy(dst[:, 4 * g:4 * g + n, :], src).then_inc(col_ok, 1)
                v.tensor_copy(val_c[0:64, k - 2, 0, 4 * g:4 * g + n, :], src[0:64])
                return v.tensor_copy(val_c[64:128, k - 2, 1, 4 * g:4 * g + n, :], src[64:128]).then_inc(col_ok, 1)

            dve.wait_ge(cols_zero, 1)
            for b in range(20):
                cols_out(b)
            link(v.tensor_tensor(fe, fe, cntR[:, 0:NC, :].unsqueeze(3).to_broadcast([NP, NC, SLOTS, FE]), ALU.mult))
            link(v.tensor_reduce(S8[:, :, :], fe.rearrange("p c s f -> p c f s"), AX, ALU.add))
            v.tensor_scalar(degr[:, :], S8[:, :, 1], 1.0, None, ALU.add).then_inc(deg_ok, 1)
            dve.wait_ge(sq_ok, 1)
            link(v.reciprocal(dinv[:, :], degr[:, :]))
            for i, k in enumerate(WT):
                dve.wait_ge(wt_ps, i + 1)
                src = ps[:, 4 + i // 4, (i % 4) * D:(i % 4) * D + D]
                if k == "L2_W":
                    link(v.tensor_tensor(WT[k][:, :], src, raw_w[:, i, :], ALU.subtract))
                    link(v.scalar_tensor_tensor(WT[k][:, :], ident[:, :], -GAMMA, WT[k][:, :], ALU.mult, ALU.add))
                else:
                    link(v.tensor_copy(WT[k][:, :], src))
            link(v.tensor_tensor(W8[0:1, :], W8[0:1, :], be_row[:, :], ALU.add))
            link(v.tensor_tensor(brow[:, 0, :], brow[:, 0, :], brow[:, 1, :], ALU.add))
            v.memset(stats[:, :, :, :], 0.0).then_inc(wt_ok, 1)

            def produce(q, u):
                b = u % 3
                cols = slice(u * TS, u * TS + TS)
                v.tensor_tensor(hot_hi[b], iota_hi,
                                hi_c[:, bass.ds(q, 1), cols].to_broadcast([128, NP, TS]), ALU.is_equal)
                v.tensor_tensor(eq_lo[b], iota_lo,
                                lo_c[:, bass.ds(q, 1), cols].to_broadcast([128, NC, TS]),
                                ALU.is_equal).then_inc(eq_ok, 1)
                dve.wait_ge(eq_ok, STEPS * q + u + 1)
                for k in range(3):
                    ins = v.tensor_tensor(
                        hot_lo[b][:, k],
                        eq_lo[b].unsqueeze(2).to_broadcast([128, NC, 2, TS]),
                        val_c[:, k, :, bass.ds(q, 1), cols].rearrange("p j a t -> p a j t").to_broadcast([128, NC, 2, TS]),
                        ALU.mult)
                ins.then_inc(hots_ok, 1)

            def lo_part(q, u):
                for h, (b0, nb) in enumerate(((0, 3), (3, 2))):
                    dve.wait_ge(unit_act, 2 * STEPS * q + 2 * u + h + 1)
                    src = ps[0:NP, b0:b0 + nb, 0:BT * 100].rearrange("p b (t k n) -> p b n k t", t=BT, k=2)[:, :, :, 1]
                    dst = [stg[:, bass.ds(q % 2, 1), m, :, u * TS + b0 * BT:u * TS + (b0 + nb) * BT]
                           .rearrange("p a n (b t) -> p (a b) n t", t=BT) for m in (1, 2)]
                    v.tensor_tensor(dst[1], src, dst[0], ALU.subtract).then_inc(unit_free, 1)

            dve.wait_ge(iotas, 1)
            dve.wait_ge(col_ok, 20)
            dve.sem_inc(unit_free, 2)
            produce(0, 0)
            with dve.Fori(0, PAIRS) as q:
                for u in range(STEPS):
                    if u < STEPS - 1:
                        produce(q, u + 1)
                    else:
                        produce(q + 1, 0)
                    lo_part(q, u)

            for g in range(GROUPS):
                n = chunks_of(g) * NP
                dve.wait_ge(rep_ps, g + 1)
                link(v.tensor_scalar(inv_deg[:, g, 0:n], ps[:, 2 + g % 2, 0:n], 1.0, None, ALU.max))
                v.reciprocal(inv_deg[:, g, 0:n], inv_deg[:, g, 0:n]).then_inc(rep_ok, 1)
            dve.wait_ge(rep_ok, GROUPS)

            lns = [0]

            def layer_norm(dst, y, i, n):
                for c in range(n):
                    ins = v.bn_stats(stats[:, i, c, :], y[:, c, :])
                link(ins)
                for c in range(n):
                    ins = v.bn_aggr(mv[:, i, c, :], stats[:, i, c, :])
                ins.then_inc(var_ready, 1)
                lns[0] += 1
                dve.wait_ge(std_ready, lns[0])
                link(v.reciprocal(rstd[:, i, 0:n], std[:, i, 0:n]))
                for c in range(n):
                    ins = v.tensor_scalar(dst[:, c, :], y[:, c, :], mv[:, i, c, 0:1], rstd[:, i, c:c + 1],
                                          ALU.subtract, ALU.mult)
                return ins

            def split(r, g, n, src):
                to = parts(r + 1)
                cs = slice(GRP * g, GRP * g + n)
                link(v.tensor_copy(to[:, 0, cs, :], src))
                if n_parts(r + 1) == 2:
                    v.tensor_tensor(to[:, 1, cs, :], src, to[:, 0, cs, :], ALU.subtract).then_inc(parts_ready, 1)
                else:
                    z = Z[g % 2][:, 0:n, :]
                    link(v.tensor_tensor(z, src, to[:, 0, cs, :], ALU.subtract))
                    link(v.tensor_copy(to[:, 1, cs, :], z))
                    v.tensor_tensor(to[:, 2, cs, :], z, to[:, 1, cs, :], ALU.subtract).then_inc(parts_ready, 1)

            def first_sum(q):
                r, g = divmod(q, GROUPS)
                n = chunks_of(g) * NP
                t1 = T1[q % 2][:, 0:n]
                pa = ps[:, q % 2, 0:n]
                xt = XT[:, GCOL * g:GCOL * g + n]
                dve.wait_ge(item_used, item_no[(r, g, 2 if layer_of(r) == 2 else 0)] + 1)
                if q >= 2:
                    dve.wait_ge(s2_done, q - 1)
                if r in (1, 2):
                    dve.wait_ge(xt_ready, GROUPS * (r - 1) + g + 1)
                if layer_of(r) == 0:
                    v.tensor_tensor(t1, xt, pa, ALU.add).then_inc(t1_ready, 1)
                elif layer_of(r) == 1:
                    link(v.tensor_tensor(t1, pa, inv_deg[:, g, 0:n], ALU.mult))
                    v.tensor_tensor(t1, t1, xt, ALU.add).then_inc(t1_ready, 1)
                else:
                    v.tensor_copy(t1, pa).then_inc(t1_ready, 1)

            def finish(q):
                r, g = divmod(q, GROUPS)
                i, n = q % 2, chunks_of(g)
                cs = slice(GRP * g, GRP * g + n)
                y, z, xn = Y[i][:, 0:n, :], Z[i][:, 0:n, :], Xn[:, cs, :]
                pb = ps[0:NP, 2 + i, :].rearrange("p (c f) -> p c f", f=D)[:, 0:n, :]
                pc = ps[0:NP, 4 + i, :].rearrange("p (c f) -> p c f", f=D)[:, 0:n, :]
                scale = dinv[:, cs].unsqueeze(2).to_broadcast([NP, n, D])

                def bias(k):
                    return brow[:, k:k + 1, :].to_broadcast([NP, n, D])

                dve.wait_ge(s2_done, q + 1)
                if r == 0:
                    v.tensor_tensor(y, pc, bias(0), ALU.add).then_inc(s2_read, 1)
                    dve.wait_ge(s2_read, q + 1)
                    link(v.tensor_tensor(y, y, xn, ALU.add))
                    layer_norm(xn, y, i, n).then_inc(v_ready, 1)
                    dve.wait_ge(v_ready, q + 1)
                    split(r, g, n, xn)
                elif r == 1:
                    if g >= 2:
                        dve.wait_ge(s3_done, q - 1)
                    v.tensor_tensor(y, pc, bias(2), ALU.add).then_inc(s2_read, 1)
                    dve.wait_ge(s2_read, q + 1)
                    v.tensor_scalar(y, y, 0.0, None, ALU.max).then_inc(v_ready, 1)
                    dve.wait_ge(v_ready, q + 1)
                    split(r, g, n, y)
                elif r == 2:
                    dve.wait_ge(s3_done, q - 1)
                    v.tensor_tensor(y, pc, bias(3), ALU.add).then_inc(s2_read, 1)
                    dve.wait_ge(s2_read, q + 1)
                    link(v.scalar_tensor_tensor(y, y, 0.0, xn, ALU.max, ALU.add))
                    layer_norm(xn, y, i, n).then_inc(v_ready, 1)
                    dve.wait_ge(v_ready, q + 1)
                    v.tensor_copy(Cn[:, cs, :], xn)
                    link(v.tensor_tensor(z, xn, scale, ALU.mult))
                    split(r, g, n, z)
                elif layer_of(r) == 2:
                    cn = Cn[:, cs, :]
                    link(v.tensor_tensor(y, pb, scale, ALU.mult))
                    v.tensor_tensor(y, y, pc, ALU.add).then_inc(s2_read, 1)
                    dve.wait_ge(s2_read, q + 1)
                    v.tensor_tensor(y, y, bias(4), ALU.add).then_inc(pre_tanh, 1)
                    dve.wait_ge(tanh_ok, q - 3 * GROUPS + 1)
                    if r < 6:
                        v.scalar_tensor_tensor(cn, z, EPS_STEP, cn, ALU.mult, ALU.add).then_inc(v_ready, 1)
                        dve.wait_ge(v_ready, q + 1)
                        link(v.tensor_tensor(z, cn, scale, ALU.mult))
                        split(r, g, n, z)
                    else:
                        link(v.scalar_tensor_tensor(cn, z, EPS_STEP, cn, ALU.mult, ALU.add))
                        link(v.tensor_tensor(y, cn, xn, ALU.add))
                        link(layer_norm(xn, y, i, n))
                        split(r, g, n, xn)
                else:
                    v.scalar_tensor_tensor(y, pc, 0.0, xn, ALU.max, ALU.add).then_inc(s2_read, 1)
                    dve.wait_ge(s2_read, q + 1)
                    if g >= 2:
                        dve.wait_ge(y_out[g % 2], 16 * (g // 2))
                    layer_norm(z, y, i, n).then_inc(y_ready, 1)

            dve.wait_ge(xt0_ok, GROUPS)
            for q in range(ROUNDS * GROUPS):
                first_sum(q)
                finish(q)

        @block.scalar
        def _(act):
            s = nc.scalar
            for g in range(GROUPS):
                n = chunks_of(g) * NP
                act.wait_ge(xt_ps, g + 1)
                s.activation(XT[:, GCOL * g:GCOL * g + n], ps[:, 6 + g % 2, 0:n], ACT.Copy).then_inc(xt0_ok, 1)
            act.wait_ge(deg_ok, 1)
            s.activation(degr[:, :], degr[:, :], ACT.Sqrt).then_inc(sq_ok, 1)

            with act.Fori(0, PAIRS) as q:
                act.wait_ge(stg_free, q + 1)
                for u in range(STEPS):
                    for h, (b0, nb) in enumerate(((0, 3), (3, 2))):
                        act.wait_ge(unit_mm, 2 * STEPS * q + 2 * u + h + 1)
                        for k in range(2):
                            src = ps[0:NP, b0:b0 + nb, 0:BT * 100].rearrange("p b (t k n) -> p b n k t", t=BT, k=2)[:, :, :, k]
                            dst = (stg[:, bass.ds(q % 2, 1), k, :, u * TS + b0 * BT:u * TS + (b0 + nb) * BT]
                                   .rearrange("p a n (b t) -> p (a b) n t", t=BT))
                            ins = s.activation(dst, src, ACT.Copy)
                        ins.then_inc(unit_act, 1)

            for g in range(GROUPS):
                n = chunks_of(g) * NP
                act.wait_ge(s8t_ps0, g + 1)
                s.activation(S8T[g % 2][:, 0:n], ps[0:FE, g % 2, 0:n], ACT.Copy).then_inc(s8t_ok0, 1)

            def relu_bias(q):
                r, g = divmod(q, GROUPS)
                n = chunks_of(g) * NP
                act.wait_ge(s1_done, q + 1)
                if q >= 2:
                    act.wait_ge(s2_done, q - 1)
                s.activation(T2[q % 2][:, 0:n], ps[:, 2 + q % 2, 0:n], ACT.Relu if r == 0 else ACT.Identity,
                             bias=bcol[:, r:r + 1]).then_inc(t2_ready, 1)

            def columns(q):
                r, g = divmod(q, GROUPS)
                n = chunks_of(g) * NP
                act.wait_ge(s3_done, q + 1)
                s.activation(XT[:, GCOL * g:GCOL * g + n], ps[:, 6 + q % 2, 0:n], ACT.Copy).then_inc(xt_ready, 1)

            lns = [0]
            for q in range(ROUNDS * GROUPS):
                r, g = divmod(q, GROUPS)
                i, n = q % 2, chunks_of(g)
                if r < 3:
                    relu_bias(q)
                if r == 7:
                    act.wait_ge(s1_done, q + 1)
                    if g >= 2:
                        act.wait_ge(s2_done, q - 1)
                    s.activation(S8T[i][:, 0:n * NP], ps[0:FE, 2 + i, 0:n * NP], ACT.Copy).then_inc(t2_ready, 1)
                if 1 <= q and (q - 1) // GROUPS < 6:
                    columns(q - 1)
                if layer_of(r) == 2:
                    act.wait_ge(pre_tanh, q - 3 * GROUPS + 1)
                    s.activation(Z[i][:, 0:n, :], Y[i][:, 0:n, :], ACT.Tanh).then_inc(tanh_ok, 1)
                if r in (0, 2, 6, 7):
                    lns[0] += 1
                    act.wait_ge(var_ready, lns[0])
                    s.activation(std[:, i, 0:n], mv[:, i, 0:n, 1], ACT.Sqrt, bias=eps_col[0:NP, :]).then_inc(std_ready, 1)

        @block.tensor
        def _(pe):
            t = nc.tensor
            pe.wait_ge(firstf_ok, 1)
            pe.wait_ge(consts, 2)
            t.matmul(ps[0:NP, 0, 0:NBLK], ones_row[:, :], blk_firstf, start=True, stop=True).then_inc(first_ps, 1)
            pe.wait_ge(x_in, 16)
            for g in range(GROUPS):
                if g >= 2:
                    pe.wait_ge(xt0_ok, g - 1)
                for c in range(chunks_of(g)):
                    ins = t.transpose(ps[:, 6 + g % 2, c * NP:c * NP + NP], Xn[:, GRP * g + c, :], ident[0:NP, 0:NP])
                ins.then_inc(xt_ps, 1)
            pe.wait_ge(w_in, 16 * 21)
            for i, k in enumerate(WT):
                t.transpose(ps[:, 4 + i // 4, (i % 4) * D:(i % 4) * D + D], raw_w[:, i, :], ident[:, :]).then_inc(wt_ps, 1)
            for b in range(20):
                k, g = divmod(b, 4)
                if k == 0:
                    pe.wait_ge(rec_ok, 1)
                if k >= 2:
                    pe.wait_ge(rec_ok, 2)
                if b >= 4:
                    pe.wait_ge(col_ok, b - 3)
                else:
                    pe.wait_ge(ptr_ok, 1)
                for j in range(min(4, PAIRS - 4 * g)):
                    q = 4 * g + j
                    ins = t.transpose(ps[:, b % 4, j * NP:j * NP + NP],
                                      rec[k][:, 2 * q:2 * q + 2, :].rearrange("p c s -> p (c s)"), ident[0:NP, 0:NP])
                ins.then_inc(col_ps, 1)

            pe.wait_ge(wt_ok, 1)
            with pe.Fori(0, PAIRS) as q:
                for u in range(STEPS):
                    b = u % 3
                    pe.wait_ge(hots_ok, STEPS * q + u + 1)
                    hot = hot_lo[b].rearrange("p k n j t -> p (k n j) t")
                    for h, (b0, nb) in enumerate(((0, 3), (3, 2))):
                        pe.wait_ge(unit_free, 2 * STEPS * q + 2 * u + h + 1)
                        for e in range(b0 * BT, (b0 + nb) * BT):
                            o = (e % BT) * 100
                            t.matmul(ps[0:NP, e // BT, o:o + 100], hot_hi[b][:, :, e], hot[:, 0:100, e],
                                     start=True, stop=False)
                            ins = t.matmul(ps[0:NP, e // BT, o + 50:o + 100], hot_hi[b][:, :, e], hot[:, 100:150, e],
                                           start=False, stop=True)
                        ins.then_inc(unit_mm, 1)

            pe.wait_ge(unit_free, 2 * BUILD + 2)
            for g in range(GROUPS):
                n = chunks_of(g)
                if g >= 2:
                    pe.wait_ge(s8t_ok0, g - 1)
                for c in range(n):
                    ins = t.transpose(ps[0:FE, g % 2, c * NP:c * NP + NP], S8[:, GRP * g + c, :], ident[0:NP, 0:NP])
                ins.then_inc(s8t_ps0, 1)
                pe.wait_ge(s8t_ok0, g + 1)
                if g >= 2:
                    pe.wait_ge(rep_ok, g - 1)
                t.matmul(ps[:, 2 + g % 2, 0:n * NP], sel0[:, :], S8T[g % 2][:, 0:n * NP],
                         start=True, stop=True).then_inc(rep_ps, 1)

            def product1(q):
                r, g = divmod(q, GROUPS)
                n = chunks_of(g)
                bank = 2 + q % 2
                if q >= 2:
                    if r <= 2 or q - 2 < 3 * GROUPS:
                        pe.wait_ge(t2_ready, q - 1)
                    elif q - 2 < 7 * GROUPS:
                        pe.wait_ge(s2_read, q - 1)
                    else:
                        pe.wait_ge(t2_ready, q - 1 - 4 * GROUPS)
                if r < 3:
                    pe.wait_ge(t1_ready, q + 1)
                    lhs = (Wn["L0_W1"], WT["L1_W1a"], WT["L1_W2a"])[r]
                    t.matmul(ps[:, bank, 0:n * NP], lhs[:, :], T1[q % 2][:, 0:n * NP],
                             start=True, stop=True).then_inc(s1_done, 1)
                elif layer_of(r) == 2:
                    pe.wait_ge(t1_ready, q + 1)
                    for c in range(n):
                        ins = t.matmul(ps[0:NP, bank, c * D:c * D + D], T1[q % 2][:, c * NP:c * NP + NP],
                                       WT["L2_Wphi"][:, :], start=True, stop=True)
                    ins.then_inc(s1_done, 1)
                else:
                    for c in range(n):
                        ins = t.transpose(ps[0:FE, bank, c * NP:c * NP + NP], S8[:, GRP * g + c, :], ident[0:NP, 0:NP])
                    ins.then_inc(s1_done, 1)

            def product2(q):
                r, g = divmod(q, GROUPS)
                n = chunks_of(g)
                if q >= 2:
                    pe.wait_ge(s2_read, q - 1)
                if r < 3:
                    pe.wait_ge(t2_ready, q + 1)
                if r == 7:
                    pe.wait_ge(t1_ready, q + 1)
                    pe.wait_ge(t2_ready, q + 1 - 4 * GROUPS)
                if layer_of(r) == 2:
                    pe.wait_ge(xt_ready, GROUPS * (r - 1) + g + 1)
                for c in range(n):
                    o = ps[0:NP, 4 + q % 2, c * D:c * D + D]
                    cols = slice(c * NP, c * NP + NP)
                    xt = XT[:, GCOL * g + c * NP:GCOL * g + c * NP + NP]
                    if r == 0:
                        terms = [(T2[q % 2][:, cols], Wn["L0_W2"]), (xt, Wn["L0_Wres"])]
                    elif layer_of(r) == 1:
                        terms = [(T2[q % 2][:, cols], WT["L1_W1b" if r == 1 else "L1_W2b"])]
                    elif layer_of(r) == 2:
                        terms = [(xt, WT["L2_W"])]
                    else:
                        terms = [(T1[q % 2][:, cols], Wn["L3_W"]), (S8T[q % 2][:, cols], W8)]
                    for i, (a, b) in enumerate(terms):
                        ins = t.matmul(o, a, b[:, :], start=(i == 0), stop=(i == len(terms) - 1))
                ins.then_inc(s2_done, 1)

            def transposes(q):
                r, g = divmod(q, GROUPS)
                pe.wait_ge(v_ready, q + 1)
                if q >= 2:
                    pe.wait_ge(xt_ready, q - 1)
                for c in range(chunks_of(g)):
                    k = GRP * g + c
                    src = Y[q % 2][:, c, :] if r == 1 else Cn[:, k, :] if layer_of(r) == 2 else Xn[:, k, :]
                    ins = t.transpose(ps[:, 6 + q % 2, c * NP:c * NP + NP], src, ident[0:NP, 0:NP])
                ins.then_inc(s3_done, 1)

            def need_parts(r, g, k_end):
                if g == 0:
                    if r == 0:
                        pe.wait_ge(parts0_ok, 1)
                    else:
                        pe.wait_ge(parts_ready, GROUPS * (r - 1) + -(-k_end // GRP))

            def aggregate(q):
                r, g = divmod(q, GROUPS)
                n = chunks_of(g) * NP
                o = ps[:, q % 2, 0:n]
                xs = parts(r)
                mine = [(r, g, m) for m in ((1, 2) if layer_of(r) == 2 else (0,))]
                if q >= 2:
                    pe.wait_ge(t1_ready, q - 1)

                def step(it, k0, loop, first, final):
                    slot = ring[item_no[it] % RING]
                    for kk in range(KCH):
                        k = k0 + kk
                        for j in range(n_parts(r)):
                            ks = bass.ds(k, 1) if loop else slice(k, k + 1)
                            rhs = (slot[:, :, ks, :] if n == GCOL else slot[:, 0:1, ks, 0:n])
                            if n == GCOL:
                                rhs = rhs.rearrange("p q a n -> p q (a n)")
                            else:
                                rhs = rhs.rearrange("p q a n -> p (q a n)")
                            lhs = xs[:, j, ks, :].rearrange("p a f -> p (a f)")
                            ins = t.matmul(o, lhs, rhs, start=(first and kk == 0 and j == 0),
                                           stop=(final and kk == KCH - 1 and j == n_parts(r) - 1))
                    return ins

                for a, it in enumerate(mine):
                    i = item_no[it]
                    pe.wait_ge(slot_in[i % RING], 16 * (i // RING + 1))
                    if a == 0:
                        need_parts(r, g, KCH)
                        step(it, 0, False, True, False)
                        if q >= 1:
                            product1(q - 1)
                        if q >= 2 and (q - 2) // GROUPS < 6:
                            transposes(q - 2)
                        need_parts(r, g, 2 * KCH)
                        step(it, KCH, False, False, False)
                        if q >= 1:
                            product2(q - 1)
                        need_parts(r, g, 4 * KCH)
                        k_from = 2 * KCH
                    else:
                        k_from = 0
                    with pe.Fori(k_from, 4 * KCH, KCH) as k0:
                        step(it, k0, True, False, False)
                    if a == 0:
                        need_parts(r, g, NC)
                    ins = step(it, 4 * KCH, False, False, a == len(mine) - 1)
                    ins.then_inc(item_used, 1)

            pe.wait_ge(rep_ok, GROUPS)
            for q in range(ROUNDS * GROUPS):
                aggregate(q)
            product1(ROUNDS * GROUPS - 1)
            product2(ROUNDS * GROUPS - 1)


_WEIGHTS = {
    "L0_W1": "L0_gnn_W1", "L0_b1": "L0_gnn_b1", "L0_W2": "L0_gnn_W2", "L0_b2": "L0_gnn_b2",
    "L0_Wres": "L0_gnn_Wres", "L0_bres": "L0_gnn_bres",
    "L1_W1a": "L1_gnn_W1a", "L1_b1a": "L1_gnn_b1a", "L1_W1b": "L1_gnn_W1b", "L1_b1b": "L1_gnn_b1b",
    "L1_W2a": "L1_gnn_W2a", "L1_b2a": "L1_gnn_b2a", "L1_W2b": "L1_gnn_W2b", "L1_b2b": "L1_gnn_b2b",
    "L2_W": "L2_gnn_W", "L2_bias": "L2_gnn_bias", "L2_Wphi": "L2_gnn_W_phi",
    "L3_W": "L3_gnn_W", "L3_b": "L3_gnn_b", "L3_We": "L3_gnn_We", "L3_be": "L3_gnn_be",
}


def kernel(**inputs):
    import numpy as np
    import concourse.bacc as bacc
    from concourse.bass_utils import run_bass_kernel_spmd

    pad = EP - EDGES
    src, dst = np.asarray(inputs["src"]), np.asarray(inputs["dst"])
    src = np.concatenate([src, np.zeros(pad, src.dtype)])
    dst = np.concatenate([dst, np.full(pad, NODES, dst.dtype)])
    attr, weight = np.asarray(inputs["edge_attr_6"]), np.asarray(inputs["edge_weight"])
    feats = np.concatenate([np.ones((EDGES, 1), weight.dtype), weight[:, None], attr], axis=1)
    feats = np.concatenate([feats, np.zeros((pad, FE), weight.dtype)])
    arrays = {
        "x": np.ascontiguousarray(inputs["x"]),
        "edge_pairs": np.ascontiguousarray(np.stack([src, dst], axis=1)),
        "dst_blocks": np.ascontiguousarray(dst.reshape(NBLK, BLOCK)),
        "edge_feats": np.ascontiguousarray(feats),
    }
    arrays.update({k: np.ascontiguousarray(inputs[name]) for k, name in _WEIGHTS.items()})
    nc = bacc.Bacc("TRN2", target_bir_lowering=False, num_devices=1)
    aps = {k: nc.dram_tensor("in_" + k, a.shape, mybir.dt.from_np(a.dtype), kind="ExternalInput").ap()
           for k, a in arrays.items()}
    out = nc.dram_tensor("out", (NODES, D), F32, kind="ExternalOutput").ap()
    build_program(nc, aps["x"], aps["edge_pairs"], aps["dst_blocks"], aps["edge_feats"],
                  {k: aps[k] for k in _WEIGHTS}, out)
    r = run_bass_kernel_spmd(nc, [{"in_" + k: a for k, a in arrays.items()}], core_ids=[0])
    return r.results[0]["out"]
```

```python
from contextlib import ExitStack

import concourse.bass as bass
from concourse import mybir

F32 = mybir.dt.float32
F16 = mybir.dt.float16
BF16 = mybir.dt.bfloat16
I32 = mybir.dt.int32
ALU = mybir.AluOpType
ACT = mybir.ActivationFunctionType
AX = mybir.AxisListType.X

NODES = 3125
EDGES = 103125
D = 128
NP = 125
NC = NODES // NP
SLOTS = 64
PAIRS = (NC + 1) // 2
BLOCK = 256
NBLK = -(-(EDGES + SLOTS) // BLOCK)
EP = NBLK * BLOCK
FE = 8
TS = 25
STEPS = NP // TS
BT = 5
BANKS = TS // BT
GRP = 4
GROUPS = -(-NC // GRP)
GCOL = GRP * NP
AHEAD = 2
CG = 5
KCH = 5
ROUNDS = 8
EPS_LN = 1e-5
GAMMA = 0.1
EPS_STEP = 0.1
WEIGHT_MAX = 1000.0
TILES = EP // 128
ORDERED = -(-EDGES // 128)
ROUND_MAGIC = 1.5 * 2 ** 23


def chunks_of(g):
    return min(GRP, NC - GRP * g)


def layer_of(r):
    return [0, 1, 1, 2, 2, 2, 2, 3][r]


def build_program(nc, x, edge_pairs, dst_blocks, edge_feats, w, out):
    ctx = ExitStack()
    with ctx:
        def sb(name, shape, dt=F32):
            return ctx.enter_context(nc.sbuf_tensor(name, shape, dt))

        def sem(name):
            return ctx.enter_context(nc.semaphore(name))

        mats = nc.dram_tensor("mats", (3, PAIRS, 128, NC * 2 * NP), F16).ap()

        ps = ctx.enter_context(nc.psum_tensor("ps", [128, 8, 512], F32))

        ident = sb("ident", [128, 128])
        x_buf = sb("x_buf", [128, 84 + NODES])
        Xn = x_buf[0:NP, 0:NC * D].rearrange("p (c f) -> p c f", f=D)
        sum0 = x_buf[:, 84:84 + NODES]
        XT = sb("XT", [D, NODES])
        parts_even = sb("parts_even", [NP, 3, NC, D], BF16)
        S8 = sb("S8", [NP, NC, FE])
        dinv = sb("dinv", [NP, NC])
        degr = sb("degr", [NP, NC])
        dval = sb("dval", [NP, NC + 1])
        eps_col = sb("eps_col", [128, 1])
        one_col = sb("one_col", [128, 1])
        inv_n = sb("inv_n", [NP, NC])
        Wn = {k: sb("sb_" + k, [D, D]) for k in ("L0_W1", "L0_W2", "L0_Wres", "L3_W")}
        WT = {k: sb("sbT_" + k, [D, D]) for k in ("L1_W1a", "L1_W1b", "L1_W2a", "L1_W2b", "L2_W", "L2_Wphi")}
        W8 = sb("W8", [FE, D])
        be_row = sb("be_row", [1, D])
        bcol = sb("bcol", [D, 3])
        brow = sb("brow", [NP, 5, D])
        stats = sb("stats", [NP, 2, GRP, 6])
        mv = sb("mv", [NP, 2, GRP, 2])
        std = sb("std", [NP, 2, GRP])
        rstd = sb("rstd", [NP, 2, GRP])
        ones_row = sb("ones_row", [1, NP])
        ptrf = sb("ptrf", [NP, NC])
        blkf = sb("blkf", [NP, NC])
        blki = sb("blki", [NP, NC], I32)
        ptr2 = sb("ptr2", [NP, NC], I32)
        ptr8 = sb("ptr8", [NP, NC], I32)

        flags = sb("flags", [128, 3])
        mode = sb("mode", [1, 1], I32)
        ARENA = 155520
        arena = sb("arena", [128, ARENA // 4])

        def at(off, parts, shape, dt=F32):
            size = 4 if dt in (F32, I32) else 2
            n = 1
            for s in shape:
                n *= s
            assert off % 4 == 0 and off + n * size <= ARENA, (off, shape)
            v = arena[0:parts, off // 4:off // 4 + -(-n * size // 4)]
            if dt != F32:
                v = v.bitcast(dt)[:, 0:n]
            names = "abcde"[:len(shape)]
            if len(shape) > 1:
                v = v.rearrange(f"p ({' '.join(names)}) -> p {' '.join(names)}",
                                **{names[i]: shape[i] for i in range(1, len(shape))})
            return v

        first_rep = at(75000, NP, [NBLK])
        blk_first = at(80000, 1, [NBLK], I32)
        blk_firstf = at(84000, 1, [NBLK])
        cmp1 = at(0, NP, [NC, NBLK])
        dblk = at(0, NP, [NC, BLOCK], I32)
        cmp2 = at(25600, NP, [NC, BLOCK])
        fe = at(0, NP, [NC, SLOTS, FE])
        sd = at(51200, NP, [NC, SLOTS, 2], I32)
        tmpR = at(64000, NP, [NC + 1, SLOTS])
        rec = [at(75000 + 6656 * i, NP, [NC + 1, SLOTS]) for i in range(5)]
        hiR, loR, cntR, w1R, w2R = rec
        w1h = at(70656, NP, [NC + 1, SLOTS], F16)
        raw_w = at(108280, D, [6, D])
        here = at(88000, 128, [ORDERED], I32)
        after = at(91232, 128, [ORDERED], I32)
        stg = at(0, 128, [2, 3, 2 * NC, NP], F16)
        hot_hi = [at(75000 + 13900 * i, 128, [128, TS], F16) for i in range(3)]
        hot_lo = [at(75000 + 13900 * i + 6400, 128, [3, NC, 2, TS], F16) for i in range(3)]
        iota_hi = at(116700, 128, [128, TS], F16)
        iota_lo = at(123100, 128, [NC, TS], F16)
        eq_lo = at(124352, 128, [NC, TS], F16)
        neg_ident = at(125604, 128, [128], F16)
        hi_c = at(127516, 128, [PAIRS + 1, NP], F16)
        lo_c = at(131016, 128, [PAIRS + 1, NP], F16)
        val_c = at(134516, 128, [3, 2, PAIRS + 1, NP], F16)
        RING = 4
        ring = [at(25000 * i, 128, [2, NC, 2 * NP], F16) for i in range(RING)]
        T1 = [at(100000 + 2000 * i, D, [GCOL]) for i in range(2)]
        T2 = [at(104000 + 2000 * i, D, [GCOL]) for i in range(2)]
        Y = [at(108000 + 2048 * i, NP, [GRP, D]) for i in range(2)]
        Z = [at(112096 + 2048 * i, NP, [GRP, D]) for i in range(2)]
        parts_odd = at(116192, NP, [2, NC, D], F16)
        Cn = at(128992, NP, [GROUPS * GRP, D])
        inv_deg = at(128992, D, [GROUPS, GRP * D])
        x_res = [at(147328 + 2048 * i, NP, [GRP, D]) for i in range(2)]
        S8T = [at(143328 + 2000 * i, FE, [GCOL]) for i in range(2)]

        g_hot = [at(12500 * i, 128, [NODES]) for i in range(2)]
        g_sum = at(25000, 128, [NODES])
        g_node = at(37500, 128, [NODES])
        g_pairs = at(50000, 128, [TILES, 2], I32)
        g_dst = at(56464, 128, [TILES])
        g_feats = at(59696, 128, [TILES, FE])
        g_rows = at(116192, NP, [NC, D])
        g_x = [at(85552 + 512 * i, 128, [D]) for i in range(2)]
        g_f8 = [at(86576 + 32 * i, 128, [FE]) for i in range(2)]
        g_idx = [at(86640 + 4 * i, 128, [1], I32) for i in range(2)]
        g_zero = at(86656, 128, [128])
        h_dram = nc.dram_tensor("h_rows", (NODES, D), F32).ap()

        def parts(r):
            if r % 2:
                return parts_odd
            return parts_even if r < 3 else parts_even[:, :, :, :].bitcast(F16)

        def n_parts(r):
            return 3 if r in (0, 2) else 2

        consts = sem("consts")
        x_in = sem("x_in")
        first_in = sem("first_in")
        w_in = sem("w_in")
        firstf_ok = sem("firstf_ok")
        first_ps = sem("first_ps")
        blk_ok = sem("blk_ok")
        dblk_in = [sem(f"dblk_in{i}") for i in range(NC // CG)]
        ptr_ok = sem("ptr_ok")
        sd_in = [sem(f"sd_in{i}") for i in range(NC // CG)]
        fe_in = [sem(f"fe_in{i}") for i in range(NC // CG)]
        rec_ok = sem("rec_ok")
        col_ps = sem("col_ps")
        col_ok = sem("col_ok")
        wt_ps = sem("wt_ps")
        wt_ok = sem("wt_ok")
        deg_ok = sem("deg_ok")
        sq_ok = sem("sq_ok")
        xt_ps = sem("xt_ps")
        xt0_ok = sem("xt0_ok")
        parts0_ok = sem("parts0_ok")
        iotas = sem("iotas")
        cols_zero = sem("cols_zero")
        dve_chain = sem("dve_chain")
        eq_ok = sem("eq_ok")
        hots_ok = sem("hots_ok")
        sums_ok = sem("sums_ok")
        hi_out = sem("hi_out")
        rest_ok = sem("rest_ok")
        bank_free = sem("bank_free")
        stg_free = sem("stg_free")
        mats_out = sem("mats_out")
        agg0_done = sem("agg0_done")
        sum0_out = sem("sum0_out")
        x_res_in = [sem(f"x_res_in{i}") for i in range(2)]
        rep_ps = sem("rep_ps")
        rep_ok = sem("rep_ok")
        order_in = sem("order_in")
        flag_ok = sem("flag_ok")
        flag_ps = sem("flag_ps")
        mode_ok = sem("mode_ok")
        g_in = sem("g_in")
        g_consts = sem("g_consts")
        g_hot_ok = sem("g_hot_ok")
        g_used = sem("g_used")
        g_idx_ok = sem("g_idx_ok")
        g_idx_seen = sem("g_idx_seen")
        g_x_in = [sem(f"g_x_in{i}") for i in range(2)]
        g_taken = sem("g_taken")
        g_s8_ps = sem("g_s8_ps")
        g_stored = sem("g_stored")
        slot_in = [sem(f"slot_in{i}") for i in range(RING)]
        item_used = sem("item_used")
        t1_ready = sem("t1_ready")
        s1_done = sem("s1_done")
        t2_ready = sem("t2_ready")
        s2_done = sem("s2_done")
        s2_read = sem("s2_read")
        pre_tanh = sem("pre_tanh")
        tanh_ok = sem("tanh_ok")
        var_ready = sem("var_ready")
        std_ready = sem("std_ready")
        v_ready = sem("v_ready")
        parts_ready = sem("parts_ready")
        s3_done = sem("s3_done")
        xt_ready = sem("xt_ready")
        y_ready = sem("y_ready")
        y_out = [sem(f"y_out{i}") for i in range(2)]

        items = [(r, g, m) for r in range(1, ROUNDS) for g in range(GROUPS)
                 for m in ((1, 2) if layer_of(r) == 2 else (0,))]
        item_no = {it: i for i, it in enumerate(items)}
        BUILD = PAIRS * STEPS

        def by_mode(eng, fast, general):
            eng.wait_ge(mode_ok, 1)
            m = eng.value_load(mode[0:1, 0:1], min_val=0, max_val=384)
            with eng.If(m == 0):
                fast()
            with eng.Else():
                general()

        block = ctx.enter_context(nc.Block())

        @block.sync
        def _(sp):
            sp.dma_start(blk_first, dst_blocks[:, 0:1].rearrange("b o -> o b"),
                         allow_slow_non_contiguous=True).then_inc(first_in, 16)
            sp.dma_start(Xn[:, :, :], x.rearrange("(p c) f -> p c f", c=NC)).then_inc(x_in, 16)
            for k, t in Wn.items():
                sp.dma_start(t[:, :], w[k]).then_inc(w_in, 16)
            for i, k in enumerate(WT):
                sp.dma_start(raw_w[:, i, :], w[k]).then_inc(w_in, 16)
            for i, k in enumerate(("L0_b1", "L1_b1a", "L1_b2a")):
                sp.dma_start(bcol[:, i:i + 1], w[k].rearrange("(d o) -> d o", o=1),
                             allow_slow_non_contiguous=True).then_inc(w_in, 16)
            for i, k in enumerate(("L0_b2", "L0_bres", "L1_b1b", "L1_b2b", "L2_bias")):
                sp.dma_start(brow[:, i, :], w[k].rearrange("(o d) -> o d", o=1).to_broadcast([NP, D])).then_inc(w_in, 16)
            sp.wait_ge(consts, 2)
            sp.dma_start(W8[0:1, :], w["L3_b"].rearrange("(o d) -> o d", o=1)).then_inc(w_in, 16)
            sp.dma_start(W8[2:FE, :], w["L3_We"]).then_inc(w_in, 16)
            sp.dma_start(be_row[:, :], w["L3_be"].rearrange("(o d) -> o d", o=1)).then_inc(w_in, 16)

            flat = dst_blocks.rearrange("a b -> (a b)")
            for i, t in enumerate((here, after)):
                sp.dma_start(t, flat[i:i + 128 * ORDERED].rearrange("(p t) -> p t", p=128)).then_inc(order_in, 16)

            def store_out(g):
                q = GROUPS * (ROUNDS - 1) + g
                sp.wait_ge(y_ready, g + 1)
                n = chunks_of(g)
                sp.dma_start(out.rearrange("(p c) f -> p c f", c=NC)[:, GRP * g:GRP * g + n, :],
                             Z[q % 2][:, 0:n, :]).then_inc(y_out[g % 2], 16)

            def stores():
                for g in range(GROUPS):
                    store_out(g)
                sp.wait_ge(y_out[0], 16 * ((GROUPS + 1) // 2))
                sp.wait_ge(y_out[1], 16 * (GROUPS // 2))

            def general():
                sp.dma_start(g_pairs, edge_pairs.rearrange("(p t) c -> p t c", t=TILES)).then_inc(g_in, 16)
                sp.dma_start(g_feats, edge_feats.rearrange("(p t) c -> p t c", t=TILES)).then_inc(g_in, 16)
                stores()

            def fast_loads():
                sp.sem_inc(stg_free, 2)
                with sp.Fori(0, PAIRS) as q:
                    sp.wait_ge(bank_free, BANKS * STEPS * q + BANKS * STEPS + BANKS)
                    for m in range(3):
                        sp.dma_start(mats[m, bass.ds(q, 1)].rearrange("a p n -> (a p) n"),
                                     stg[:, bass.ds(q % 2, 1), m].rearrange("p a j n -> p (a j n)")).then_inc(mats_out, 16)
                    sp.wait_ge(mats_out, 48 * q + 48)
                    sp.sem_inc(stg_free, 1)

                sp.wait_ge(sum0_out, PAIRS + 1)
                for i, (r, g, m) in enumerate(items):
                    if i >= RING:
                        sp.wait_ge(item_used, i - RING + 1)
                    n = 2 if g < GROUPS - 1 else 1
                    sp.dma_start(ring[i % RING][:, 0:n, :, :].rearrange("p q k n -> p q (k n)"),
                                 mats[m, 2 * g:2 * g + n].rearrange("q p n -> p q n")).then_inc(slot_in[i % RING], 16)
                stores()

            by_mode(sp, fast_loads, general)


        @block.gpsimd
        def _(pool):
            nc.gpsimd.memset(ident[:, :], 0.0)
            nc.gpsimd.memset(eps_col[:, :], EPS_LN)
            nc.gpsimd.memset(one_col[:, :], 1.0)
            nc.gpsimd.memset(ones_row[:, :], 1.0)
            nc.gpsimd.iota(dval[:, :], [[1, NC + 1]], base=0, channel_multiplier=NC,
                           allow_small_or_imprecise_dtypes=True)
            nc.gpsimd.memset(W8[:, :], 0.0).then_inc(consts, 1)
            pool.wait_ge(consts, 1)
            nc.gpsimd.affine_select(out=ident[:, :], in_=ident[:, :], compare_op=ALU.not_equal, fill=1.0,
                                    base=0, pattern=[[-1, 128]], channel_multiplier=1).then_inc(consts, 1)
            nc.gpsimd.iota(iota_hi, [[1, 128], [0, TS]], base=0, channel_multiplier=0,
                           allow_small_or_imprecise_dtypes=True)
            nc.gpsimd.iota(iota_lo, [[1, NC], [0, TS]], base=0, channel_multiplier=0,
                           allow_small_or_imprecise_dtypes=True).then_inc(iotas, 1)
            nc.gpsimd.memset(hi_c, 0.0)
            nc.gpsimd.memset(lo_c, 0.0)
            nc.gpsimd.memset(val_c, 0.0).then_inc(cols_zero, 1)

            pool.wait_ge(blk_ok, 1)
            for c in range(NC):
                nc.gpsimd.indirect_dma_start(dblk[:, c, :], None, dst_blocks,
                                             bass.IndirectOffsetOnAxis(blki[:, c:c + 1], 0)).then_inc(dblk_in[c // CG], 16)
            pairs_v = edge_pairs.rearrange("(a b) t -> a (b t)", b=SLOTS)
            feats_v = edge_feats.rearrange("(a b) t -> a (b t)", b=SLOTS)
            for c in range(NC):
                if c % CG == 0:
                    pool.wait_ge(ptr_ok, c // CG + 1)
                nc.gpsimd.indirect_dma_start(sd[:, c].rearrange("p s t -> p (s t)"), None, pairs_v,
                                             bass.IndirectOffsetOnAxis(ptr2[:, c:c + 1], 1)).then_inc(sd_in[c // CG], 16)
            for c in range(NC):
                nc.gpsimd.indirect_dma_start(fe[:, c].rearrange("p s t -> p (s t)"), None, feats_v,
                                             bass.IndirectOffsetOnAxis(ptr8[:, c:c + 1], 1)).then_inc(fe_in[c // CG], 16)

            def general():
                nc.gpsimd.iota(g_node, [[1, NC], [NC, NP]], base=0, channel_multiplier=0,
                               allow_small_or_imprecise_dtypes=True)
                nc.gpsimd.memset(g_zero, 0.0).then_inc(g_consts, 1)
                pool.wait_ge(g_in, 32)
                for r in range(ROUNDS):
                    if r:
                        pool.wait_ge(parts_ready, GROUPS * r)
                        pool.dma_start(h_dram.rearrange("(p c) f -> p c f", c=NC), g_rows).then_inc(g_stored, 16)
                        pool.wait_ge(g_stored, 16 * r)
                    with pool.Fori(0, TILES // 2) as i:
                        for j in range(2):
                            tile = TILES * r + 2 * i + j
                            pool.wait_ge(g_used, tile + TILES + 1)
                            nc.gpsimd.tensor_copy(g_idx[j], g_pairs[:, bass.ds(2 * i + j, 1), 0]).then_inc(g_idx_ok, 1)
                            pool.wait_ge(g_idx_ok, tile + 1)
                            pool.sem_inc(g_idx_seen, 1)
                            nc.gpsimd.indirect_dma_start(g_x[j], None, h_dram if r else x,
                                                         bass.IndirectOffsetOnAxis(g_idx[j], 0)).then_inc(g_x_in[j], 16)

            def fast():
                pool.wait_ge(sum0_out, PAIRS + 1)
                for g in range(GROUPS):
                    if g >= 2:
                        pool.wait_ge(v_ready, g - 1)
                    n = chunks_of(g)
                    pool.dma_start(x_res[g % 2][:, 0:n, :],
                                   x.rearrange("(p c) f -> p c f", c=NC)[:, GRP * g:GRP * g + n, :]).then_inc(x_res_in[g % 2], 16)

            by_mode(pool, fast, general)

        @block.vector
        def _(dve):
            v = nc.vector
            chain = [0]

            def link(ins):
                ins.then_inc(dve_chain, 1)
                chain[0] += 1
                dve.wait_ge(dve_chain, chain[0])

            dve.wait_ge(first_in, 16)
            v.tensor_copy(blk_firstf, blk_first).then_inc(firstf_ok, 1)
            dve.wait_ge(first_ps, 1)
            dve.wait_ge(consts, 2)
            link(v.tensor_copy(first_rep, ps[0:NP, 0, 0:NBLK]))
            d_c = dval[:, 0:NC].unsqueeze(2)
            link(v.tensor_tensor(cmp1, first_rep.unsqueeze(1).to_broadcast([NP, NC, NBLK]),
                                 d_c.to_broadcast([NP, NC, NBLK]), ALU.is_lt))
            link(v.tensor_reduce(blkf[:, :], cmp1, AX, ALU.add))
            link(v.tensor_scalar(blkf[:, :], blkf[:, :], -1.0, 0.0, ALU.add, ALU.max))
            v.tensor_copy(blki[:, :], blkf[:, :]).then_inc(blk_ok, 1)

            dve.wait_ge(order_in, 32)
            link(v.memset(flags[:, :], 0.0))
            link(v.tensor_tensor(after, after, here, ALU.subtract))
            link(v.tensor_reduce(flags[:, 0:1], after, AX, ALU.min))
            link(v.tensor_scalar(flags[:, 0:1], flags[:, 0:1], 0.0, None, ALU.is_lt))

            dve.wait_ge(x_in, 16)
            link(v.tensor_copy(parts_even[:, 0], Xn[:, :, :]))
            rest = at(51200, NP, [NC, D])
            link(v.tensor_tensor(rest, Xn[:, :, :], parts_even[:, 0], ALU.subtract))
            link(v.tensor_copy(parts_even[:, 1], rest))
            v.tensor_tensor(parts_even[:, 2], rest, parts_even[:, 1], ALU.subtract).then_inc(parts0_ok, 1)
            dve.wait_ge(parts0_ok, 1)

            dve.wait_ge(wt_ps, len(WT))
            for i, k in enumerate(WT):
                src = ps[:, 4 + i // 4, (i % 4) * D:(i % 4) * D + D]
                if k == "L2_W":
                    link(v.tensor_tensor(WT[k][:, :], src, raw_w[:, i, :], ALU.subtract))
                    link(v.scalar_tensor_tensor(WT[k][:, :], ident[:, :], -GAMMA, WT[k][:, :], ALU.mult, ALU.add))
                else:
                    link(v.tensor_copy(WT[k][:, :], src))
            link(v.tensor_tensor(W8[0:1, :], W8[0:1, :], be_row[:, :], ALU.add))
            link(v.tensor_tensor(brow[:, 0, :], brow[:, 0, :], brow[:, 1, :], ALU.add))
            v.memset(stats[:, :, :, :], 0.0).then_inc(wt_ok, 1)
            dve.wait_ge(wt_ok, 1)

            for i in range(NC // CG):
                cs = slice(CG * i, CG * i + CG)
                dve.wait_ge(dblk_in[i], 16 * CG)
                link(v.tensor_tensor(cmp2[:, cs], dblk[:, cs], d_c[:, cs].to_broadcast([NP, CG, BLOCK]), ALU.is_lt))
                link(v.tensor_reduce(ptrf[:, cs], cmp2[:, cs], AX, ALU.add))
                link(v.scalar_tensor_tensor(ptrf[:, cs], blkf[:, cs], float(BLOCK), ptrf[:, cs], ALU.mult, ALU.add))
                link(v.tensor_scalar(ptrf[:, cs], ptrf[:, cs], float(EP - SLOTS), None, ALU.min))
                v.tensor_scalar(ptr2[:, cs], ptrf[:, cs], 2.0, None, ALU.mult)
                v.tensor_scalar(ptr8[:, cs], ptrf[:, cs], float(FE), None, ALU.mult).then_inc(ptr_ok, 1)

            last = SLOTS - 1
            for r_ in rec[:4]:
                ins = v.memset(r_, 0.0)
            link(ins)
            for i in range(NC // CG):
                cs = slice(CG * i, CG * i + CG)
                dve.wait_ge(sd_in[i], 16 * CG)
                v.tensor_tensor(cntR[:, cs, :], sd[:, cs, :, 1], d_c[:, cs].to_broadcast([NP, CG, SLOTS]), ALU.is_equal)
                link(v.tensor_copy(hiR[:, cs, :], sd[:, cs, :, 0]))
                link(v.tensor_copy(hiR[:, cs, last], dval[:, cs]))
                link(v.tensor_scalar(tmpR[:, cs], hiR[:, cs], 1.0 / NC, -0.5 + 0.5 / NC, ALU.mult, ALU.add))
                link(v.tensor_scalar(tmpR[:, cs], tmpR[:, cs], ROUND_MAGIC, -ROUND_MAGIC, ALU.add, ALU.add))
                link(v.scalar_tensor_tensor(loR[:, cs], tmpR[:, cs], -float(NC), hiR[:, cs], ALU.mult, ALU.add))
                link(v.tensor_copy(hiR[:, cs], tmpR[:, cs]))
            link(v.tensor_reduce(flags[0:NP, 1:2], cntR[:, 0:NC, last], AX, ALU.max))
            v.memset(cntR[:, :, last], 0.0).then_inc(rec_ok, 1)
            dve.wait_ge(rec_ok, 1)
            for i in range(NC // CG):
                cs = slice(CG * i, CG * i + CG)
                dve.wait_ge(fe_in[i], 16 * CG)
                link(v.tensor_tensor(fe[:, cs], fe[:, cs], cntR[:, cs, :].unsqueeze(3).to_broadcast([NP, CG, SLOTS, FE]), ALU.mult))
                v.tensor_reduce(S8[:, cs, :], fe[:, cs].rearrange("p c s f -> p c f s"), AX, ALU.add)
                link(v.tensor_copy(w1R[:, cs, :], fe[:, cs, :, 1]))
            link(v.memset(w1R[:, 0:NC, last], 1.0))
            link(v.tensor_copy(w1h, w1R))
            link(v.tensor_tensor(w2R, w1R, w1h, ALU.subtract))
            v.tensor_copy(w1R, w1h).then_inc(rec_ok, 1)
            dve.wait_ge(rec_ok, 2)
            link(v.tensor_reduce(flags[0:NP, 2:3], w1R.rearrange("p c s -> p (c s)"), AX, ALU.max, apply_absolute_value=True))
            link(v.tensor_scalar(flags[0:NP, 2:3], flags[0:NP, 2:3], WEIGHT_MAX, None, ALU.is_gt))
            v.tensor_reduce(flags[:, 0:1], flags[:, :], AX, ALU.max).then_inc(flag_ok, 1)
            def degrees():
                link(v.tensor_scalar(inv_n[:, :], S8[:, :, 0], 1.0, None, ALU.max))
                link(v.reciprocal(inv_n[:, :], inv_n[:, :]))
                v.tensor_scalar(degr[:, :], S8[:, :, 1], 1.0, None, ALU.add).then_inc(deg_ok, 1)

            degrees()

            dve.wait_ge(flag_ps, 1)
            v.tensor_copy(mode[:, :], ps[0:1, 6, 0:1]).then_inc(mode_ok, 1)

            def produce(q, u):
                b = u % 3
                cols = slice(u * TS, u * TS + TS)
                dve.wait_ge(sums_ok, BANKS * (STEPS * q + u + 1))
                v.tensor_tensor(hot_hi[b], iota_hi,
                                hi_c[:, bass.ds(q, 1), cols].to_broadcast([128, 128, TS]), ALU.is_equal)
                dve.wait_ge(hots_ok, STEPS * q + u + 1)
                v.tensor_tensor(eq_lo, iota_lo,
                                lo_c[:, bass.ds(q, 1), cols].to_broadcast([128, NC, TS]),
                                ALU.is_equal).then_inc(eq_ok, 1)
                dve.wait_ge(eq_ok, STEPS * q + u + 1)
                for k in range(3):
                    ins = v.tensor_tensor(
                        hot_lo[b][:, k],
                        eq_lo.unsqueeze(2).to_broadcast([128, NC, 2, TS]),
                        val_c[:, k, :, bass.ds(q, 1), cols].rearrange("p j a t -> p a j t").to_broadcast([128, NC, 2, TS]),
                        ALU.mult)
                ins.then_inc(hots_ok, 1)

            lns = [0]

            def layer_norm(dst, y, i, n):
                for c in range(n):
                    ins = v.bn_stats(stats[:, i, c, :], y[:, c, :])
                link(ins)
                for c in range(n):
                    ins = v.bn_aggr(mv[:, i, c, :], stats[:, i, c, :])
                ins.then_inc(var_ready, 1)
                lns[0] += 1
                dve.wait_ge(std_ready, lns[0])
                link(v.reciprocal(rstd[:, i, 0:n], std[:, i, 0:n]))
                for c in range(n):
                    ins = v.tensor_scalar(dst[:, c, :], y[:, c, :], mv[:, i, c, 0:1], rstd[:, i, c:c + 1],
                                          ALU.subtract, ALU.mult)
                return ins

            def split(r, g, n, src, general):
                if general:
                    if r and g == 0:
                        dve.wait_ge(g_stored, 16 * r)
                    v.tensor_copy(g_rows[:, GRP * g:GRP * g + n, :], src).then_inc(parts_ready, 1)
                    dve.wait_ge(parts_ready, GROUPS * r + g + 1)
                    return
                to = parts(r + 1)
                cs = slice(GRP * g, GRP * g + n)
                link(v.tensor_copy(to[:, 0, cs, :], src))
                if n_parts(r + 1) == 2:
                    v.tensor_tensor(to[:, 1, cs, :], src, to[:, 0, cs, :], ALU.subtract).then_inc(parts_ready, 1)
                else:
                    z = Z[g % 2][:, 0:n, :]
                    link(v.tensor_tensor(z, src, to[:, 0, cs, :], ALU.subtract))
                    link(v.tensor_copy(to[:, 1, cs, :], z))
                    v.tensor_tensor(to[:, 2, cs, :], z, to[:, 1, cs, :], ALU.subtract).then_inc(parts_ready, 1)

            def first_sum(q, general):
                r, g = divmod(q, GROUPS)
                n = chunks_of(g) * NP
                if r == 0 and not general:
                    dve.sem_inc(t1_ready, 1)
                    return
                t1 = T1[q % 2][:, 0:n]
                pa = g_sum[:, GCOL * g:GCOL * g + n] if general else ps[:, q % 2, 0:n]
                xt = XT[:, GCOL * g:GCOL * g + n]
                if not general:
                    dve.wait_ge(item_used, item_no[(r, g, 2 if layer_of(r) == 2 else 0)] + 1)
                if q >= 2:
                    dve.wait_ge(s2_done, q - 1)
                if r in (1, 2):
                    dve.wait_ge(rep_ok, g + 1)
                    dve.wait_ge(xt_ready, GROUPS * (r - 1) + g + 1)
                if layer_of(r) == 0:
                    v.tensor_tensor(t1, xt, pa, ALU.add).then_inc(t1_ready, 1)
                elif layer_of(r) == 1:
                    link(v.tensor_tensor(t1, pa, inv_deg[:, g, 0:n], ALU.mult))
                    v.tensor_tensor(t1, t1, xt, ALU.add).then_inc(t1_ready, 1)
                else:
                    v.tensor_copy(t1, pa).then_inc(t1_ready, 1)

            def finish(q, general):
                r, g = divmod(q, GROUPS)
                i, n = q % 2, chunks_of(g)
                cs = slice(GRP * g, GRP * g + n)
                y, z, xn = Y[i][:, 0:n, :], Z[i][:, 0:n, :], Xn[:, cs, :]
                pb = ps[0:NP, 2 + i, :].rearrange("p (c f) -> p c f", f=D)[:, 0:n, :]
                pc = ps[0:NP, 4 + i, :].rearrange("p (c f) -> p c f", f=D)[:, 0:n, :]
                scale = dinv[:, cs].unsqueeze(2).to_broadcast([NP, n, D])

                def bias(k):
                    return brow[:, k:k + 1, :].to_broadcast([NP, n, D])

                dve.wait_ge(s2_done, q + 1)
                if r == 0:
                    v.tensor_tensor(y, pc, bias(0), ALU.add).then_inc(s2_read, 1)
                    dve.wait_ge(s2_read, q + 1)
                    if not general:
                        dve.wait_ge(x_res_in[i], 16 * (g // 2 + 1))
                    link(v.tensor_tensor(y, y, xn if general else x_res[i][:, 0:n, :], ALU.add))
                    layer_norm(xn, y, i, n).then_inc(v_ready, 1)
                    dve.wait_ge(v_ready, q + 1)
                    split(r, g, n, xn, general)
                elif r == 1:
                    if g >= 2:
                        dve.wait_ge(s3_done, q - 1)
                    v.tensor_tensor(y, pc, bias(2), ALU.add).then_inc(s2_read, 1)
                    dve.wait_ge(s2_read, q + 1)
                    v.tensor_scalar(y, y, 0.0, None, ALU.max).then_inc(v_ready, 1)
                    dve.wait_ge(v_ready, q + 1)
                    split(r, g, n, y, general)
                elif r == 2:
                    dve.wait_ge(s3_done, q - 1)
                    v.tensor_tensor(y, pc, bias(3), ALU.add).then_inc(s2_read, 1)
                    dve.wait_ge(s2_read, q + 1)
                    link(v.scalar_tensor_tensor(y, y, 0.0, xn, ALU.max, ALU.add))
                    layer_norm(xn, y, i, n).then_inc(v_ready, 1)
                    dve.wait_ge(v_ready, q + 1)
                    v.tensor_copy(Cn[:, cs, :], xn)
                    link(v.tensor_tensor(z, xn, scale, ALU.mult))
                    split(r, g, n, z, general)
                elif layer_of(r) == 2:
                    cn = Cn[:, cs, :]
                    link(v.tensor_tensor(y, pb, scale, ALU.mult))
                    v.tensor_tensor(y, y, pc, ALU.add).then_inc(s2_read, 1)
                    dve.wait_ge(s2_read, q + 1)
                    v.tensor_tensor(y, y, bias(4), ALU.add).then_inc(pre_tanh, 1)
                    dve.wait_ge(tanh_ok, q - 3 * GROUPS + 1)
                    if r < 6:
                        v.scalar_tensor_tensor(cn, z, EPS_STEP, cn, ALU.mult, ALU.add).then_inc(v_ready, 1)
                        dve.wait_ge(v_ready, q + 1)
                        link(v.tensor_tensor(z, cn, scale, ALU.mult))
                        split(r, g, n, z, general)
                    else:
                        link(v.scalar_tensor_tensor(cn, z, EPS_STEP, cn, ALU.mult, ALU.add))
                        link(v.tensor_tensor(y, cn, xn, ALU.add))
                        link(layer_norm(xn, y, i, n))
                        split(r, g, n, xn, general)
                else:
                    v.scalar_tensor_tensor(y, pc, 0.0, xn, ALU.max, ALU.add).then_inc(s2_read, 1)
                    dve.wait_ge(s2_read, q + 1)
                    if g >= 2:
                        dve.wait_ge(y_out[g % 2], 16 * (g // 2))
                    layer_norm(z, y, i, n).then_inc(y_ready, 1)

            def fast():
                dve.wait_ge(iotas, 1)
                v.tensor_scalar(neg_ident, ident[:, :], -1.0, None, ALU.mult).then_inc(hots_ok, 1)
                dve.wait_ge(col_ok, 20)
                with dve.Fori(0, PAIRS) as q:
                    for u in range(STEPS):
                        produce(q, u)
                dve.wait_ge(sq_ok, 1)
                link(v.reciprocal(dinv[:, :], degr[:, :]))
                dve.wait_ge(xt0_ok, GROUPS)
                for q in range(ROUNDS * GROUPS):
                    first_sum(q, False)
                    finish(q, False)

            def general():
                dve.wait_ge(g_in, 32)
                dve.wait_ge(col_ok, 20)
                dve.wait_ge(g_consts, 1)
                link(v.tensor_copy(g_dst, g_pairs[:, :, 1]))

                def one_hots(a, m):
                    with dve.Fori(0, TILES // 2) as i:
                        for j in range(2):
                            tile = bass.ds(2 * i + j, 1)
                            dve.wait_ge(g_used, TILES * a + 2 * i + j + 1)
                            if a == 0:
                                v.tensor_copy(g_f8[j], g_feats[:, tile, :].rearrange("p a f -> p (a f)"))
                            v.tensor_scalar(g_hot[j], g_node, g_dst[:, tile], g_feats[:, tile, m],
                                            ALU.is_equal, ALU.mult).then_inc(g_hot_ok, 1)

                def take(a, n_part):
                    dve.wait_ge(g_used, TILES * (a + 1) + 2)
                    for g in range(GROUPS):
                        n = chunks_of(g) * NP
                        ins = v.tensor_copy(g_sum[0:n_part, GCOL * g:GCOL * g + n], ps[0:n_part, g, 0:n])
                    ins.then_inc(g_taken, 1)
                    dve.wait_ge(g_taken, a + 1)

                one_hots(0, 0)
                take(0, FE)
                dve.wait_ge(g_s8_ps, 1)
                link(v.tensor_copy(S8[:, :, :], ps[0:NP, 7, 0:NC * FE].rearrange("p (c f) -> p c f", f=FE)))
                dve.wait_ge(sq_ok, 1)
                degrees()
                dve.wait_ge(sq_ok, 2)
                link(v.reciprocal(dinv[:, :], degr[:, :]))
                dve.wait_ge(xt0_ok, GROUPS)
                for r in range(ROUNDS):
                    one_hots(r + 1, 1 if layer_of(r) == 2 else 0)
                    take(r + 1, 128)
                    for q in range(GROUPS * r, GROUPS * r + GROUPS):
                        first_sum(q, True)
                        finish(q, True)

            def count_again(path):
                def run():
                    at_branch = chain[0], lns[0]
                    path()
                    chain[0], lns[0] = at_branch
                return run

            by_mode(dve, count_again(fast), count_again(general))

        @block.scalar
        def _(act):
            s = nc.scalar
            for g in range(GROUPS):
                n = chunks_of(g) * NP
                act.wait_ge(xt_ps, g + 1)
                s.activation(XT[:, GCOL * g:GCOL * g + n], ps[:, 6 + g % 2, 0:n], ACT.Copy).then_inc(xt0_ok, 1)
            act.wait_ge(cols_zero, 1)
            for b in range(20):
                """The slots' columns leave PSUM: (record, four pairs); each chunk in its half."""
                k, g = divmod(b, 4)
                n = min(4, PAIRS - 4 * g)
                act.wait_ge(col_ps, b + 1)
                src = ps[:, b % 4, 0:n * NP].rearrange("p (q t) -> p q t", t=NP)
                if k < 2:
                    ins = s.activation((hi_c, lo_c)[k][:, 4 * g:4 * g + n, :], src, ACT.Copy)
                else:
                    for j in range(2):
                        ins = s.activation(val_c[64 * j:64 * j + 64, k - 2, j, 4 * g:4 * g + n, :],
                                           src[64 * j:64 * j + 64], ACT.Copy)
                ins.then_inc(col_ok, 1)
            act.wait_ge(deg_ok, 1)
            s.activation(degr[:, :], degr[:, :], ACT.Sqrt).then_inc(sq_ok, 1)

            def relu_bias(q):
                r, g = divmod(q, GROUPS)
                n = chunks_of(g) * NP
                act.wait_ge(s1_done, q + 1)
                if q >= 2:
                    act.wait_ge(s2_done, q - 1)
                s.activation(T2[q % 2][:, 0:n], ps[:, 2 + q % 2, 0:n], ACT.Relu if r == 0 else ACT.Identity,
                             bias=bcol[:, r:r + 1]).then_inc(t2_ready, 1)

            def columns(q):
                r, g = divmod(q, GROUPS)
                n = chunks_of(g) * NP
                act.wait_ge(s3_done, q + 1)
                s.activation(XT[:, GCOL * g:GCOL * g + n], ps[:, 6 + q % 2, 0:n], ACT.Copy).then_inc(xt_ready, 1)

            def fast():
                def pair(q, first=False):
                    act.wait_ge(stg_free, q + 1)
                    act.wait_ge(agg0_done, q + 1)

                    def leave(i, low):
                        done = BANKS * STEPS * q + i + 1
                        act.wait_ge(rest_ok if low else sums_ok, done if low else done + AHEAD * BANKS)
                        src = ps[:, i % BANKS, 0:BT * 100].rearrange("p (t k n) -> p k n t", t=BT, k=2)[:, low:2]
                        dst = stg[:, bass.ds(q % 2, 1), 2 * low:2 + low, :, i * BT:i * BT + BT].rearrange("p a k n t -> p (a k) n t")
                        s.activation(dst, src, ACT.Copy).then_inc(bank_free if low else hi_out, 1)

                    for i in range(BANKS * STEPS):
                        leave(i, 0)
                        if i:
                            leave(i - 1, 1)
                    leave(BANKS * STEPS - 1, 1)
                    if not first:
                        sum_out(q - 1, 2 * NP)

                def sum_out(q, n):
                    act.wait_ge(agg0_done, q + 3)
                    s.activation(sum0[:, bass.ds(q * (2 * NP), n)], ps[:, BANKS, 0:n], ACT.Copy).then_inc(sum0_out, 1)

                act.sem_inc(sum0_out, 1)
                pair(0, first=True)
                with act.Fori(1, PAIRS) as q:
                    pair(q)
                sum_out(PAIRS - 1, NP)

                after_build(False)

            def general():
                act.wait_ge(deg_ok, 2)
                s.activation(degr[:, :], degr[:, :], ACT.Sqrt).then_inc(sq_ok, 1)
                after_build(True)

            def after_build(general):
                for g in range(GROUPS):
                    n = chunks_of(g) * NP
                    act.wait_ge(rep_ps, g + 1)
                    s.activation(inv_deg[:, g, 0:n], ps[:, g % 2, 0:n], ACT.Copy).then_inc(rep_ok, 1)

                lns = [0]
                for q in range(ROUNDS * GROUPS):
                    r, g = divmod(q, GROUPS)
                    i, n = q % 2, chunks_of(g)
                    if r < 3:
                        relu_bias(q)
                    if r == 7:
                        act.wait_ge(s1_done, q + 1)
                        if g >= 2:
                            act.wait_ge(s2_done, q - 1)
                        s.activation(S8T[i][:, 0:n * NP], ps[0:FE, 2 + i, 0:n * NP], ACT.Copy).then_inc(t2_ready, 1)
                    if not general and 1 <= q and (q - 1) // GROUPS < 6:
                        columns(q - 1)
                    if layer_of(r) == 2:
                        act.wait_ge(pre_tanh, q - 3 * GROUPS + 1)
                        s.activation(Z[i][:, 0:n, :], Y[i][:, 0:n, :], ACT.Tanh).then_inc(tanh_ok, 1)
                    if r in (0, 2, 6, 7):
                        lns[0] += 1
                        act.wait_ge(var_ready, lns[0])
                        s.activation(std[:, i, 0:n], mv[:, i, 0:n, 1], ACT.Sqrt, bias=eps_col[0:NP, :]).then_inc(std_ready, 1)
                    if general and r < 6:
                        columns(q)

            by_mode(act, fast, general)

        @block.tensor
        def _(pe):
            t = nc.tensor
            pe.wait_ge(firstf_ok, 1)
            pe.wait_ge(consts, 2)
            t.matmul(ps[0:NP, 0, 0:NBLK], ones_row[:, :], blk_firstf, start=True, stop=True).then_inc(first_ps, 1)
            pe.wait_ge(x_in, 16)
            for g in range(GROUPS):
                if g >= 2:
                    pe.wait_ge(xt0_ok, g - 1)
                for c in range(chunks_of(g)):
                    ins = t.transpose(ps[:, 6 + g % 2, c * NP:c * NP + NP], Xn[:, GRP * g + c, :], ident[0:NP, 0:NP])
                ins.then_inc(xt_ps, 1)
            pe.wait_ge(w_in, 16 * 21)
            for i, k in enumerate(WT):
                t.transpose(ps[:, 4 + i // 4, (i % 4) * D:(i % 4) * D + D], raw_w[:, i, :], ident[:, :]).then_inc(wt_ps, 1)
            for b in range(20):
                k, g = divmod(b, 4)
                if k == 0:
                    pe.wait_ge(rec_ok, 1)
                if k >= 3:
                    pe.wait_ge(rec_ok, 2)
                if b >= 4:
                    pe.wait_ge(col_ok, b - 3)
                else:
                    pe.wait_ge(ptr_ok, 1)
                for j in range(min(4, PAIRS - 4 * g)):
                    q = 4 * g + j
                    ins = t.transpose(ps[:, b % 4, j * NP:j * NP + NP],
                                      rec[k][:, 2 * q:2 * q + 2, :].rearrange("p c s -> p (c s)"), ident[0:NP, 0:NP])
                ins.then_inc(col_ps, 1)

            def product1(q, general=False):
                r, g = divmod(q, GROUPS)
                n = chunks_of(g)
                bank = 2 + q % 2
                if q >= 2:
                    if r <= 2 or q - 2 < 3 * GROUPS:
                        pe.wait_ge(t2_ready, q - 1)
                    elif q - 2 < 7 * GROUPS:
                        pe.wait_ge(s2_read, q - 1)
                    else:
                        pe.wait_ge(t2_ready, q - 1 - 4 * GROUPS)
                if r < 3:
                    if r or general:
                        pe.wait_ge(t1_ready, q + 1)
                    lhs = (Wn["L0_W1"], WT["L1_W1a"], WT["L1_W2a"])[r]
                    rhs = T1[q % 2][:, 0:n * NP] if r or general else sum0[:, GCOL * g:GCOL * g + n * NP]
                    t.matmul(ps[:, bank, 0:n * NP], lhs[:, :], rhs, start=True, stop=True).then_inc(s1_done, 1)
                elif layer_of(r) == 2:
                    pe.wait_ge(t1_ready, q + 1)
                    for c in range(n):
                        ins = t.matmul(ps[0:NP, bank, c * D:c * D + D], T1[q % 2][:, c * NP:c * NP + NP],
                                       WT["L2_Wphi"][:, :], start=True, stop=True)
                    ins.then_inc(s1_done, 1)
                else:
                    for c in range(n):
                        ins = t.transpose(ps[0:FE, bank, c * NP:c * NP + NP], S8[:, GRP * g + c, :], ident[0:NP, 0:NP])
                    ins.then_inc(s1_done, 1)

            def product2(q):
                r, g = divmod(q, GROUPS)
                n = chunks_of(g)
                if q >= 2:
                    pe.wait_ge(s2_read, q - 1)
                if r < 3:
                    pe.wait_ge(t2_ready, q + 1)
                if r == 7:
                    pe.wait_ge(t1_ready, q + 1)
                    pe.wait_ge(t2_ready, q + 1 - 4 * GROUPS)
                if layer_of(r) == 2:
                    pe.wait_ge(xt_ready, GROUPS * (r - 1) + g + 1)
                for c in range(n):
                    o = ps[0:NP, 4 + q % 2, c * D:c * D + D]
                    cols = slice(c * NP, c * NP + NP)
                    xt = XT[:, GCOL * g + c * NP:GCOL * g + c * NP + NP]
                    if r == 0:
                        terms = [(T2[q % 2][:, cols], Wn["L0_W2"]), (xt, Wn["L0_Wres"])]
                    elif layer_of(r) == 1:
                        terms = [(T2[q % 2][:, cols], WT["L1_W1b" if r == 1 else "L1_W2b"])]
                    elif layer_of(r) == 2:
                        terms = [(xt, WT["L2_W"])]
                    else:
                        terms = [(T1[q % 2][:, cols], Wn["L3_W"]), (S8T[q % 2][:, cols], W8)]
                    for i, (a, b) in enumerate(terms):
                        ins = t.matmul(o, a, b[:, :], start=(i == 0), stop=(i == len(terms) - 1))
                ins.then_inc(s2_done, 1)

            def transposes(q):
                r, g = divmod(q, GROUPS)
                pe.wait_ge(v_ready, q + 1)
                if q >= 2:
                    pe.wait_ge(xt_ready, q - 1)
                for c in range(chunks_of(g)):
                    k = GRP * g + c
                    src = Y[q % 2][:, c, :] if r == 1 else Cn[:, k, :] if layer_of(r) == 2 else Xn[:, k, :]
                    ins = t.transpose(ps[:, 6 + q % 2, c * NP:c * NP + NP], src, ident[0:NP, 0:NP])
                ins.then_inc(s3_done, 1)

            def need_parts(r, g, k_end):
                if g == 0:
                    if r == 0:
                        pe.wait_ge(parts0_ok, 1)
                    else:
                        pe.wait_ge(parts_ready, GROUPS * (r - 1) + -(-k_end // GRP))

            def aggregate(q):
                r, g = divmod(q, GROUPS)
                n = chunks_of(g) * NP
                o = ps[:, q % 2, 0:n]
                xs = parts(r)
                mine = [(r, g, m) for m in ((1, 2) if layer_of(r) == 2 else (0,))]
                if q >= 2:
                    pe.wait_ge(t1_ready, q - 1)

                def step(it, k0, loop, first, final):
                    slot = ring[item_no[it] % RING][0:NP]
                    for kk in range(KCH):
                        k = k0 + kk
                        for j in range(n_parts(r)):
                            ks = bass.ds(k, 1) if loop else slice(k, k + 1)
                            rhs = (slot[:, :, ks, :] if n == GCOL else slot[:, 0:1, ks, 0:n])
                            if n == GCOL:
                                rhs = rhs.rearrange("p q a n -> p q (a n)")
                            else:
                                rhs = rhs.rearrange("p q a n -> p (q a n)")
                            lhs = xs[:, j, ks, :].rearrange("p a f -> p (a f)")
                            ins = t.matmul(o, lhs, rhs, start=(first and kk == 0 and j == 0),
                                           stop=(final and kk == KCH - 1 and j == n_parts(r) - 1))
                    return ins

                for a, it in enumerate(mine):
                    i = item_no[it]
                    pe.wait_ge(slot_in[i % RING], 16 * (i // RING + 1))
                    if a == 0:
                        need_parts(r, g, KCH)
                        step(it, 0, False, True, False)
                        if q >= 1:
                            product1(q - 1)
                        if q >= 2 and (q - 2) // GROUPS < 6:
                            transposes(q - 2)
                        need_parts(r, g, 2 * KCH)
                        step(it, KCH, False, False, False)
                        if q >= 1:
                            product2(q - 1)
                        need_parts(r, g, 4 * KCH)
                        k_from = 2 * KCH
                    else:
                        k_from = 0
                    with pe.Fori(k_from, 4 * KCH, KCH) as k0:
                        step(it, k0, True, False, False)
                    if a == 0:
                        need_parts(r, g, NC)
                    ins = step(it, 4 * KCH, False, False, a == len(mine) - 1)
                    ins.then_inc(item_used, 1)

            pe.wait_ge(flag_ok, 1)
            pe.wait_ge(xt0_ok, GROUPS)
            t.matmul(ps[0:1, 6, 0:1], flags[:, 0:1], one_col[:, :], start=True, stop=True).then_inc(flag_ps, 1)

            def spread_degrees():
                for g in range(GROUPS):
                    if g >= 2:
                        pe.wait_ge(rep_ok, g - 1)
                    for c in range(chunks_of(g)):
                        k = GRP * g + c
                        ins = t.matmul(ps[:, g % 2, c * NP:c * NP + NP], inv_n[:, k:k + 1].to_broadcast([NP, 128]),
                                       ident[0:NP, 0:NP], start=True, stop=True)
                    ins.then_inc(rep_ps, 1)
                pe.wait_ge(rep_ok, GROUPS)

            def fast():
                pe.wait_ge(wt_ok, 1)
                pe.wait_ge(parts0_ok, 1)
                pe.sem_inc(sums_ok, AHEAD * BANKS)
                pe.sem_inc(bank_free, BANKS)
                pe.sem_inc(agg0_done, 2)

                def sum_counts(q, ks, n):
                    o = ps[:, BANKS, 0:n]
                    for k in ks:
                        if k == 0:
                            pe.wait_ge(sum0_out, q + 1)
                        for j in range(3):
                            rhs = stg[0:NP, bass.ds(q % 2, 1), 0, 2 * k:2 * k + n // NP, :].rearrange("p a n t -> p (a n t)")
                            t.matmul(o, parts_even[:, j, k, :], rhs, start=(k == 0 and j == 0), stop=False,
                                     skip_group_check=True)
                        if k == NC - 1:
                            t.matmul(o, ident[:, :], XT[:, bass.ds(q * (2 * NP), n)], start=False, stop=True,
                                     skip_group_check=True).then_inc(agg0_done, 1)

                def pair(q, first=False):
                    def take_high(i):
                        pe.wait_ge(hi_out, BANKS * STEPS * q + i + 1)
                        o = ps[:, i % BANKS, 0:BT * 100].rearrange("p (t k n) -> p k t n", t=BT, k=2)[:, 1]
                        high = stg[:, bass.ds(q % 2, 1), 1, :, i * BT:i * BT + BT].rearrange("p a n t -> p (a t) n")
                        t.matmul(o, neg_ident, high, start=False, stop=True, skip_group_check=True).then_inc(rest_ok, 1)

                    for u in range(STEPS):
                        b = u % 3
                        pe.wait_ge(hots_ok, STEPS * q + u + 2)
                        hot = hot_lo[b].rearrange("p k n j t -> p (k n j) t")
                        for bank in range(BANKS):
                            i = BANKS * u + bank
                            pe.wait_ge(bank_free, BANKS * STEPS * q + i + 1)
                            for e in range(BT):
                                o = e * 100
                                T = bank * BT + e
                                t.matmul(ps[:, bank, o:o + 100], hot_hi[b][:, :, T], hot[:, 0:100, T],
                                         start=(e == 0), stop=False, skip_group_check=True)
                                ins = t.matmul(ps[:, bank, o + 50:o + 100], hot_hi[b][:, :, T], hot[:, 100:150, T],
                                               start=False, stop=(e == BT - 1), skip_group_check=True)
                            ins.then_inc(sums_ok, 1)
                            if i:
                                take_high(i - 1)
                            if not first and u:
                                a, z = ((BANKS * (u - 1) + bank + d) * NC // (BANKS * (STEPS - 1)) for d in (0, 1))
                                sum_counts(q - 1, range(a, z), 2 * NP)
                    take_high(BANKS * STEPS - 1)

                pair(0, first=True)
                with pe.Fori(1, PAIRS) as q:
                    pair(q)
                sum_counts(PAIRS - 1, range(NC), NP)
                pe.wait_ge(bank_free, BANKS * BUILD + BANKS)
                spread_degrees()
                pe.wait_ge(sum0_out, PAIRS + 1)
                product1(0)
                for g in range(1, GROUPS):
                    if g < GROUPS - 1:
                        product1(g)
                    product2(g - 1)
                    if g >= 2:
                        transposes(g - 2)
                for q in range(GROUPS, ROUNDS * GROUPS):
                    aggregate(q)
                product1(ROUNDS * GROUPS - 1)
                product2(ROUNDS * GROUPS - 1)

            def general():
                pe.wait_ge(wt_ok, 1)
                pe.wait_ge(col_ok, 20)
                pe.wait_ge(g_consts, 1)
                pe.sem_inc(g_used, 2)

                def sums(a, lhs, n_part, own_rows):
                    for g in range(GROUPS):
                        n = chunks_of(g) * NP
                        t.matmul(ps[0:n_part, g, 0:n], g_zero[:, 0:n_part], g_node[:, GCOL * g:GCOL * g + n],
                                 start=True, stop=False, skip_group_check=True)
                    if own_rows:
                        for c in range(NC):
                            o = (c % GRP) * NP
                            t.matmul(ps[:, c // GRP, o:o + NP], g_rows[:, c, :], ident[0:NP, 0:NP],
                                     start=False, stop=False, skip_group_check=True)
                    with pe.Fori(0, TILES // 2) as i:
                        for j in range(2):
                            pe.wait_ge(g_hot_ok, TILES * a + 2 * i + j + 1)
                            if a:
                                pe.wait_ge(g_x_in[j], 8 * TILES * (a - 1) + 16 * i + 16)
                            for g in range(GROUPS):
                                n = chunks_of(g) * NP
                                ins = t.matmul(ps[0:n_part, g, 0:n], lhs[j], g_hot[j][:, GCOL * g:GCOL * g + n],
                                               start=False, stop=False, skip_group_check=True)
                            ins.then_inc(g_used, 1)

                pe.wait_ge(parts0_ok, 1)
                sums(0, g_f8, FE, False)
                pe.wait_ge(g_taken, 1)
                for c in range(NC):
                    ins = t.transpose(ps[0:NP, 7, c * FE:c * FE + FE], g_sum[0:FE, c * NP:c * NP + NP], ident[0:FE, 0:FE])
                ins.then_inc(g_s8_ps, 1)
                pe.wait_ge(deg_ok, 2)
                spread_degrees()
                for r in range(ROUNDS):
                    if r:
                        pe.wait_ge(s2_read, GROUPS * r)
                        pe.wait_ge(xt_ready, GROUPS * min(r, 6))
                        pe.wait_ge(parts_ready, GROUPS * r)
                    sums(r + 1, g_x, 128, layer_of(r) == 2)
                    pe.wait_ge(g_taken, r + 2)
                    for q in range(GROUPS * r, GROUPS * r + GROUPS):
                        product1(q, general=True)
                        product2(q)
                        if r < 6:
                            transposes(q)

            by_mode(pe, fast, general)


_WEIGHTS = {
    "L0_W1": "L0_gnn_W1", "L0_b1": "L0_gnn_b1", "L0_W2": "L0_gnn_W2", "L0_b2": "L0_gnn_b2",
    "L0_Wres": "L0_gnn_Wres", "L0_bres": "L0_gnn_bres",
    "L1_W1a": "L1_gnn_W1a", "L1_b1a": "L1_gnn_b1a", "L1_W1b": "L1_gnn_W1b", "L1_b1b": "L1_gnn_b1b",
    "L1_W2a": "L1_gnn_W2a", "L1_b2a": "L1_gnn_b2a", "L1_W2b": "L1_gnn_W2b", "L1_b2b": "L1_gnn_b2b",
    "L2_W": "L2_gnn_W", "L2_bias": "L2_gnn_bias", "L2_Wphi": "L2_gnn_W_phi",
    "L3_W": "L3_gnn_W", "L3_b": "L3_gnn_b", "L3_We": "L3_gnn_We", "L3_be": "L3_gnn_be",
}


def kernel(**inputs):
    import numpy as np
    import concourse.bacc as bacc
    from concourse.bass_utils import run_bass_kernel_spmd

    pad = EP - EDGES
    src, dst = np.asarray(inputs["src"]), np.asarray(inputs["dst"])
    src = np.concatenate([src, np.zeros(pad, src.dtype)])
    dst = np.concatenate([dst, np.full(pad, NODES, dst.dtype)])
    attr, weight = np.asarray(inputs["edge_attr_6"]), np.asarray(inputs["edge_weight"])
    feats = np.concatenate([np.ones((EDGES, 1), weight.dtype), weight[:, None], attr], axis=1)
    feats = np.concatenate([feats, np.zeros((pad, FE), weight.dtype)])
    arrays = {
        "x": np.ascontiguousarray(inputs["x"]),
        "edge_pairs": np.ascontiguousarray(np.stack([src, dst], axis=1)),
        "dst_blocks": np.ascontiguousarray(dst.reshape(NBLK, BLOCK)),
        "edge_feats": np.ascontiguousarray(feats),
    }
    arrays.update({k: np.ascontiguousarray(inputs[name]) for k, name in _WEIGHTS.items()})
    nc = bacc.Bacc("TRN2", target_bir_lowering=False, num_devices=1)
    aps = {k: nc.dram_tensor("in_" + k, a.shape, mybir.dt.from_np(a.dtype), kind="ExternalInput").ap()
           for k, a in arrays.items()}
    out = nc.dram_tensor("out", (NODES, D), F32, kind="ExternalOutput").ap()
    build_program(nc, aps["x"], aps["edge_pairs"], aps["dst_blocks"], aps["edge_feats"],
                  {k: aps[k] for k in _WEIGHTS}, out)
    r = run_bass_kernel_spmd(nc, [{"in_" + k: a for k, a in arrays.items()}], core_ids=[0])
    return r.results[0]["out"]
```

```python
from contextlib import ExitStack

import concourse.bass as bass
from concourse import mybir

F32 = mybir.dt.float32
F16 = mybir.dt.float16
BF16 = mybir.dt.bfloat16
I32 = mybir.dt.int32
ALU = mybir.AluOpType
ACT = mybir.ActivationFunctionType
AX = mybir.AxisListType.X

NODES = 3125
EDGES = 103125
D = 128
NP = 125
NC = NODES // NP
SLOTS = 64
PAIRS = (NC + 1) // 2
BT4 = 4
BLOCK = 256
NBLK = -(-(EDGES + SLOTS) // BLOCK)
EP = NBLK * BLOCK
FE = 8
TS = 25
STEPS = NP // TS
BT = 5
BANKS = TS // BT
GRP = 4
GROUPS = -(-NC // GRP)
GCOL = GRP * NP
LAG = 2
AHEAD = 2
CG = 5
KCH = 5
ROUNDS = 8
EPS_LN = 1e-5
GAMMA = 0.1
EPS_STEP = 0.1
WEIGHT_MAX = 1000.0
L1_MAX = 1.0
TILES = EP // 128
ORDERED = -(-EDGES // 128)
ROUND_MAGIC = 1.5 * 2 ** 23


def chunks_of(g):
    return min(GRP, NC - GRP * g)


def layer_of(r):
    return [0, 1, 1, 2, 2, 2, 2, 3][r]


def build_program(nc, x, edge_pairs, edge_w, dst_blocks, edge_feats, w, out):
    ctx = ExitStack()
    with ctx:
        def sb(name, shape, dt=F32):
            return ctx.enter_context(nc.sbuf_tensor(name, shape, dt))

        def sem(name):
            return ctx.enter_context(nc.semaphore(name))

        mats = nc.dram_tensor("mats", (3, PAIRS, 128, NC * 2 * NP), F16).ap()

        table = nc.dram_tensor("edge_table", (EP, 3), F32).ap()

        ps = ctx.enter_context(nc.psum_tensor("ps", [128, 8, 512], F32))

        ident = sb("ident", [128, 128])
        x_buf = sb("x_buf", [128, 84 + NODES])
        Xn = x_buf[0:NP, 0:NC * D].rearrange("p (c f) -> p c f", f=D)
        sum0 = x_buf[:, 84:84 + NODES]
        XT = sb("XT", [D, NODES])
        parts_even = sb("parts_even", [NP, 3, NC, D], BF16)
        S8 = sb("S8", [NP, NC, FE])
        dinv = sb("dinv", [NP, NC])
        degr = sb("degr", [NP, NC])
        dval = sb("dval", [NP, NC + 1])
        eps_col = sb("eps_col", [128, 1])
        one_col = sb("one_col", [128, 1])
        inv_n = sb("inv_n", [NP, NC])
        Wn = {k: sb("sb_" + k, [D, D]) for k in ("L0_W1", "L0_W2", "L0_Wres", "L3_W")}
        WT = {k: sb("sbT_" + k, [D, D]) for k in ("L1_W1a", "L1_W1b", "L1_W2a", "L1_W2b", "L2_W", "L2_Wphi")}
        W8 = sb("W8", [FE, D])
        be_row = sb("be_row", [1, D])
        bcol = sb("bcol", [D, 3])
        brow = sb("brow", [NP, 5, D])
        stats = sb("stats", [NP, 2, GRP, 6])
        mv = sb("mv", [NP, 2, GRP, 2])
        std = sb("std", [NP, 2, GRP])
        rstd = sb("rstd", [NP, 2, GRP])
        ptrf = sb("ptrf", [NP, NC])
        blkf = sb("blkf", [NP, NC])
        blki = sb("blki", [NP, NC], I32)
        ptr3 = sb("ptr3", [NP, NC], I32)
        ptr8 = sb("ptr8", [NP, NC], I32)

        flags = sb("flags", [128, 4])
        mode = sb("mode", [1, 1], I32)
        ARENA = 155520
        arena = sb("arena", [128, ARENA // 4])

        def at(off, parts, shape, dt=F32):
            size = 4 if dt in (F32, I32) else 2
            n = 1
            for s in shape:
                n *= s
            assert off % 4 == 0 and off + n * size <= ARENA, (off, shape)
            v = arena[0:parts, off // 4:off // 4 + -(-n * size // 4)]
            if dt != F32:
                v = v.bitcast(dt)[:, 0:n]
            names = "abcde"[:len(shape)]
            if len(shape) > 1:
                v = v.rearrange(f"p ({' '.join(names)}) -> p {' '.join(names)}",
                                **{names[i]: shape[i] for i in range(1, len(shape))})
            return v

        blk_first = at(82000, NBLK // BT4, [BT4], I32)
        blk_firstf = at(82016, NBLK // BT4, [BT4])
        blk_ones = at(82032, NBLK // BT4, [1], F16)
        node_no = at(75000, NBLK // BT4, [NC, NP], F16)
        before = at(0, NBLK // BT4, [BT4, NC, NP], F16)
        dblk = at(0, NP, [NC, BLOCK], I32)
        cmp2 = at(25600, NP, [NC, BLOCK])
        t_rows = at(51200, 128, [TILES, 3])
        t_pairs = at(60896, 128, [TILES, 2], I32)
        t_w = at(67360, 128, [TILES])
        sdw = at(51200, NP, [NC, SLOTS, 3])
        w_slots = at(0, NP, [NC, SLOTS])
        rest = at(25600, NP, [NC, D])
        rec = [at(75000 + 6656 * i, NP, [NC + 1, SLOTS]) for i in range(5)]
        hiR, loR, w1R, w2R, cntR = rec
        w1h = at(70656, NP, [NC + 1, SLOTS], F16)
        raw_w = at(108280, D, [6, D])
        here = at(88000, 128, [ORDERED], I32)
        after = at(91232, 128, [ORDERED], I32)
        stg = at(0, 128, [2, 3, 2 * NC, NP], F16)
        hot_hi = [at(75000 + 13900 * i, 128, [128, TS], F16) for i in range(3)]
        hot_lo = [at(75000 + 13900 * i + 6400, 128, [3, 2 * NC, TS], F16) for i in range(3)]
        iota_hi = at(116700, 128, [128, TS], F16)
        iota_lo = at(123100, 128, [2 * NC, TS], F16)
        neg_ident = at(125604, 128, [128], F16)
        hi_c = at(127516, 128, [PAIRS + 1, NP], F16)
        lo_c = at(131016, 128, [PAIRS + 1, NP], F16)
        w_c = at(134516, 128, [2, PAIRS + 1, NP], F16)
        code_base = at(141516, 128, [1])
        attrs = [at(147328 + 2048 * i, NP, [SLOTS, FE]) for i in range(3)]
        slot_no = at(153472, NP, [SLOTS])
        slot_used = at(153728, NP, [SLOTS])
        w_max = at(153984, NP, [NC // CG])
        l1_max = at(154004, 128, [6])
        RING = 4
        ring = [at(25000 * i, 128, [2, NC, 2 * NP], F16) for i in range(RING)]
        T1 = [at(100000 + 2000 * i, D, [GCOL]) for i in range(2)]
        T2 = [at(104000 + 2000 * i, D, [GCOL]) for i in range(2)]
        Y = [at(108000 + 2048 * i, NP, [GRP, D]) for i in range(2)]
        Z = [at(112096 + 2048 * i, NP, [GRP, D]) for i in range(2)]
        parts_odd = at(116192, NP, [2, NC, D], F16)
        Cn = at(128992, NP, [GROUPS * GRP, D])
        inv_deg = at(128992, D, [GROUPS, GRP * D])
        S8T = [at(143328 + 2000 * i, FE, [GCOL]) for i in range(2)]

        g_hot = [at(12500 * i, 128, [NODES]) for i in range(2)]
        g_sum = at(25000, 128, [NODES])
        g_node = at(37500, 128, [NODES])
        g_pairs = at(50000, 128, [TILES, 2], I32)
        g_dst = at(56464, 128, [TILES])
        g_feats = at(59696, 128, [TILES, FE])
        g_rows = at(116192, NP, [NC, D])
        g_x = [at(85552 + 512 * i, 128, [D]) for i in range(2)]
        g_f8 = [at(86576 + 32 * i, 128, [FE]) for i in range(2)]
        g_idx = [at(86640 + 4 * i, 128, [1], I32) for i in range(2)]
        g_zero = at(86656, 128, [128])
        h_dram = nc.dram_tensor("h_rows", (NODES, D), F32).ap()

        def parts(r):
            if r % 2:
                return parts_odd
            return parts_even if r == 0 else parts_even[:, :, :, :].bitcast(F16)

        def n_parts(r):
            return 3 if r == 0 else 2

        consts = sem("consts")
        x_in = sem("x_in")
        first_in = sem("first_in")
        w_in = sem("w_in")
        first_ps = sem("first_ps")
        blk_ok = sem("blk_ok")
        dblk_in = [sem(f"dblk_in{i}") for i in range(NC // CG)]
        ptr_ok = sem("ptr_ok")
        sd_in = [sem(f"sd_in{i}") for i in range(NC // CG)]
        attrs_in = [sem(f"attrs_in{i}") for i in range(3)]
        attrs_ok = sem("attrs_ok")
        node_no_ok = sem("node_no_ok")
        before_ok = sem("before_ok")
        table_in = sem("table_in")
        table_ok = sem("table_ok")
        table_out = sem("table_out")
        rec_ok = sem("rec_ok")
        col_ps = sem("col_ps")
        col_ok = sem("col_ok")
        wt_ps = sem("wt_ps")
        wt_ok = sem("wt_ok")
        deg_ok = sem("deg_ok")
        sq_ok = sem("sq_ok")
        xt_ps = sem("xt_ps")
        xt0_ok = sem("xt0_ok")
        parts0_ok = sem("parts0_ok")
        round_ok = sem("round_ok")
        rest0_ok = sem("rest0_ok")
        iotas = sem("iotas")
        cols_zero = sem("cols_zero")
        dve_chain = sem("dve_chain")
        eq_ok = sem("eq_ok")
        hots_ok = sem("hots_ok")
        sums_ok = sem("sums_ok")
        hi_out = sem("hi_out")
        rest_ok = sem("rest_ok")
        bank_free = sem("bank_free")
        stg_free = sem("stg_free")
        mats_out = sem("mats_out")
        agg0_done = sem("agg0_done")
        sum0_out = sem("sum0_out")
        rep_ps = sem("rep_ps")
        rep_ok = sem("rep_ok")
        order_in = sem("order_in")
        flag_ok = sem("flag_ok")
        flag_ps = sem("flag_ps")
        mode_ok = sem("mode_ok")
        g_in = sem("g_in")
        g_consts = sem("g_consts")
        g_hot_ok = sem("g_hot_ok")
        g_used = sem("g_used")
        g_idx_ok = sem("g_idx_ok")
        g_idx_seen = sem("g_idx_seen")
        g_x_in = [sem(f"g_x_in{i}") for i in range(2)]
        g_taken = sem("g_taken")
        g_s8_ps = sem("g_s8_ps")
        g_stored = sem("g_stored")
        slot_in = [sem(f"slot_in{i}") for i in range(RING)]
        item_used = sem("item_used")
        t1_ready = sem("t1_ready")
        s1_done = sem("s1_done")
        t2_ready = sem("t2_ready")
        s2_done = sem("s2_done")
        s2_read = sem("s2_read")
        pre_tanh = sem("pre_tanh")
        tanh_ok = sem("tanh_ok")
        var_ready = sem("var_ready")
        std_ready = sem("std_ready")
        v_ready = sem("v_ready")
        parts_ready = sem("parts_ready")
        s3_done = sem("s3_done")
        xt_ready = sem("xt_ready")
        y_ready = sem("y_ready")
        y_out = [sem(f"y_out{i}") for i in range(2)]

        items = [(r, g, m) for r in range(1, ROUNDS) for g in range(GROUPS)
                 for m in ((1, 2) if layer_of(r) == 2 else (0,))]
        item_no = {it: i for i, it in enumerate(items)}
        BUILD = PAIRS * STEPS

        def by_mode(eng, fast, general):
            eng.wait_ge(mode_ok, 1)
            m = eng.value_load(mode[0:1, 0:1], min_val=0, max_val=384)
            with eng.If(m == 0):
                fast()
            with eng.Else():
                general()

        block = ctx.enter_context(nc.Block())

        @block.sync
        def _(sp):
            sp.dma_start(blk_first, dst_blocks[:, 0:1].rearrange("(p a) o -> p (a o)", a=BT4),
                         allow_slow_non_contiguous=True).then_inc(first_in, 16)
            sp.dma_start(t_pairs, edge_pairs.rearrange("(p t) c -> p t c", t=TILES)).then_inc(table_in, 16)
            sp.dma_start(t_w, edge_w.rearrange("(p t) -> p t", t=TILES)).then_inc(table_in, 16)
            sp.dma_start(Xn[:, :, :], x.rearrange("(p c) f -> p c f", c=NC)).then_inc(x_in, 16)
            for k, t in Wn.items():
                sp.dma_start(t[:, :], w[k]).then_inc(w_in, 16)
            for i, k in enumerate(WT):
                sp.dma_start(raw_w[:, i, :], w[k]).then_inc(w_in, 16)
            for i, k in enumerate(("L0_b1", "L1_b1a", "L1_b2a")):
                sp.dma_start(bcol[:, i:i + 1], w[k].rearrange("(d o) -> d o", o=1),
                             allow_slow_non_contiguous=True).then_inc(w_in, 16)
            for i, k in enumerate(("L0_b2", "L0_bres", "L1_b1b", "L1_b2b", "L2_bias")):
                sp.dma_start(brow[:, i, :], w[k].rearrange("(o d) -> o d", o=1).to_broadcast([NP, D])).then_inc(w_in, 16)
            sp.wait_ge(consts, 2)
            sp.dma_start(W8[0:1, :], w["L3_b"].rearrange("(o d) -> o d", o=1)).then_inc(w_in, 16)
            sp.dma_start(W8[2:FE, :], w["L3_We"]).then_inc(w_in, 16)
            sp.dma_start(be_row[:, :], w["L3_be"].rearrange("(o d) -> o d", o=1)).then_inc(w_in, 16)

            flat = dst_blocks.rearrange("a b -> (a b)")
            for i, t in enumerate((here, after)):
                sp.dma_start(t, flat[i:i + 128 * ORDERED].rearrange("(p t) -> p t", p=128)).then_inc(order_in, 16)

            sp.wait_ge(table_ok, 1)
            sp.dma_start(table.rearrange("(p t) c -> p t c", t=TILES), t_rows).then_inc(table_out, 16)

            def store_out(g):
                q = GROUPS * (ROUNDS - 1) + g
                sp.wait_ge(y_ready, g + 1)
                n = chunks_of(g)
                sp.dma_start(out.rearrange("(p c) f -> p c f", c=NC)[:, GRP * g:GRP * g + n, :],
                             Z[q % 2][:, 0:n, :]).then_inc(y_out[g % 2], 16)

            def stores():
                for g in range(GROUPS):
                    store_out(g)
                sp.wait_ge(y_out[0], 16 * ((GROUPS + 1) // 2))
                sp.wait_ge(y_out[1], 16 * (GROUPS // 2))

            def general():
                sp.dma_start(g_pairs, edge_pairs.rearrange("(p t) c -> p t c", t=TILES)).then_inc(g_in, 16)
                sp.dma_start(g_feats, edge_feats.rearrange("(p t) c -> p t c", t=TILES)).then_inc(g_in, 16)
                stores()

            def fast_loads():
                sp.sem_inc(stg_free, 2)
                with sp.Fori(0, PAIRS) as q:
                    sp.wait_ge(bank_free, BANKS * STEPS * q + BANKS * STEPS + BANKS)
                    for m in range(3):
                        sp.dma_start(mats[m, bass.ds(q, 1)].rearrange("a p n -> (a p) n"),
                                     stg[:, bass.ds(q % 2, 1), m].rearrange("p a j n -> p (a j n)")).then_inc(mats_out, 16)
                    sp.wait_ge(mats_out, 48 * q + 48)
                    sp.sem_inc(stg_free, 1)

                sp.wait_ge(sum0_out, PAIRS + 1)
                for i, (r, g, m) in enumerate(items):
                    if i >= RING:
                        sp.wait_ge(item_used, i - RING + 1)
                    n = 2 if g < GROUPS - 1 else 1
                    sp.dma_start(ring[i % RING][:, 0:n, :, :].rearrange("p q k n -> p q (k n)"),
                                 mats[m, 2 * g:2 * g + n].rearrange("q p n -> p q n")).then_inc(slot_in[i % RING], 16)
                stores()

            by_mode(sp, fast_loads, general)


        @block.gpsimd
        def _(pool):
            nc.gpsimd.iota(node_no, [[1, NC], [NC, NP]], base=-(NODES // 2), channel_multiplier=0,
                           allow_small_or_imprecise_dtypes=True)
            nc.gpsimd.memset(blk_ones, 1.0).then_inc(node_no_ok, 1)
            nc.gpsimd.memset(ident[:, :], 0.0)
            nc.gpsimd.memset(eps_col[:, :], EPS_LN)
            nc.gpsimd.memset(one_col[:, :], 1.0)
            nc.gpsimd.iota(dval[:, :], [[1, NC + 1]], base=0, channel_multiplier=NC,
                           allow_small_or_imprecise_dtypes=True)
            nc.gpsimd.memset(W8[:, :], 0.0).then_inc(consts, 1)
            pool.wait_ge(consts, 1)
            nc.gpsimd.affine_select(out=ident[:, :], in_=ident[:, :], compare_op=ALU.not_equal, fill=1.0,
                                    base=0, pattern=[[-1, 128]], channel_multiplier=1).then_inc(consts, 1)
            pool.wait_ge(blk_ok, 1)
            for c in range(NC):
                nc.gpsimd.indirect_dma_start(dblk[:, c, :], None, dst_blocks,
                                             bass.IndirectOffsetOnAxis(blki[:, c:c + 1], 0)).then_inc(dblk_in[c // CG], 16)
            table_v = table.rearrange("(a b) t -> a (b t)", b=SLOTS)
            pool.wait_ge(table_out, 16)
            for c in range(NC):
                if c % CG == 0:
                    pool.wait_ge(ptr_ok, c // CG + 1)
                nc.gpsimd.indirect_dma_start(sdw[:, c].rearrange("p s t -> p (s t)"), None, table_v,
                                             bass.IndirectOffsetOnAxis(ptr3[:, c:c + 1], 1)).then_inc(sd_in[c // CG], 16)

            nc.gpsimd.iota(slot_no, [[1, SLOTS]], base=0, channel_multiplier=0,
                           allow_small_or_imprecise_dtypes=True)
            nc.gpsimd.iota(iota_hi, [[1, 128], [0, TS]], base=0, channel_multiplier=0,
                           allow_small_or_imprecise_dtypes=True)
            nc.gpsimd.iota(iota_lo, [[1, 2 * NC], [0, TS]], base=0, channel_multiplier=0,
                           allow_small_or_imprecise_dtypes=True).then_inc(iotas, 1)

            def general():
                nc.gpsimd.iota(g_node, [[1, NC], [NC, NP]], base=0, channel_multiplier=0,
                               allow_small_or_imprecise_dtypes=True)
                nc.gpsimd.memset(g_zero, 0.0).then_inc(g_consts, 1)
                pool.wait_ge(g_in, 32)
                for r in range(ROUNDS):
                    if r:
                        pool.wait_ge(parts_ready, GROUPS * r)
                        pool.dma_start(h_dram.rearrange("(p c) f -> p c f", c=NC), g_rows).then_inc(g_stored, 16)
                        pool.wait_ge(g_stored, 16 * r)
                    with pool.Fori(0, TILES // 2) as i:
                        for j in range(2):
                            tile = TILES * r + 2 * i + j
                            pool.wait_ge(g_used, tile + TILES + 1)
                            nc.gpsimd.tensor_copy(g_idx[j], g_pairs[:, bass.ds(2 * i + j, 1), 0]).then_inc(g_idx_ok, 1)
                            pool.wait_ge(g_idx_ok, tile + 1)
                            pool.sem_inc(g_idx_seen, 1)
                            nc.gpsimd.indirect_dma_start(g_x[j], None, h_dram if r else x,
                                                         bass.IndirectOffsetOnAxis(g_idx[j], 0)).then_inc(g_x_in[j], 16)

            def fast():
                feats_v = edge_feats.rearrange("(a b) t -> a (b t)", b=SLOTS)
                for c in range(NC):
                    if c >= 3:
                        pool.wait_ge(attrs_ok, c - 2)
                    nc.gpsimd.indirect_dma_start(attrs[c % 3].rearrange("p s t -> p (s t)"), None, feats_v,
                                                 bass.IndirectOffsetOnAxis(ptr8[:, c:c + 1], 1)).then_inc(attrs_in[c % 3], 16)

            by_mode(pool, fast, general)

        @block.vector
        def _(dve):
            v = nc.vector
            chain = [0]

            def link(ins):
                ins.then_inc(dve_chain, 1)
                chain[0] += 1
                dve.wait_ge(dve_chain, chain[0])

            dve.wait_ge(first_in, 16)
            link(v.tensor_scalar(blk_firstf, blk_first, -float(NODES // 2), None, ALU.add))
            dve.wait_ge(node_no_ok, 1)
            for a in range(BT4):
                v.tensor_scalar(before[:, a], node_no, blk_firstf[:, a:a + 1], None, ALU.is_gt).then_inc(before_ok, 1)
            dve.wait_ge(table_in, 32)
            v.tensor_copy(t_rows[:, :, 0:2], t_pairs)
            v.tensor_copy(t_rows[:, :, 2], t_w).then_inc(table_ok, 1)
            v.memset(hi_c, 0.0)
            v.memset(lo_c, -1.0)
            v.memset(w_c, 0.0).then_inc(cols_zero, 1)
            d_c = dval[:, 0:NC].unsqueeze(2)
            dve.wait_ge(first_ps, 1)
            link(v.tensor_scalar(blkf[:, :], ps[0:NP, 0, 0:NC], -1.0, 0.0, ALU.add, ALU.max))
            v.tensor_copy(blki[:, :], blkf[:, :]).then_inc(blk_ok, 1)

            dve.wait_ge(consts, 2)
            dve.wait_ge(order_in, 32)
            link(v.memset(flags[:, :], 0.0))
            link(v.tensor_tensor(after, after, here, ALU.subtract))
            link(v.tensor_reduce(flags[:, 0:1], after, AX, ALU.min))
            link(v.tensor_scalar(flags[:, 0:1], flags[:, 0:1], 0.0, None, ALU.is_lt))

            dve.wait_ge(x_in, 16)
            dve.wait_ge(round_ok, 1)
            v.tensor_tensor(rest, Xn[:, :, :], parts_even[:, 0], ALU.subtract).then_inc(rest0_ok, 1)

            dve.wait_ge(wt_ps, len(WT))
            for i, k in enumerate(WT):
                src = ps[:, 4 + i // 4, (i % 4) * D:(i % 4) * D + D]
                if k == "L2_W":
                    link(v.tensor_tensor(WT[k][:, :], src, raw_w[:, i, :], ALU.subtract))
                    link(v.scalar_tensor_tensor(WT[k][:, :], ident[:, :], -GAMMA, WT[k][:, :], ALU.mult, ALU.add))
                else:
                    link(v.tensor_copy(WT[k][:, :], src))
            link(v.tensor_tensor(W8[0:1, :], W8[0:1, :], be_row[:, :], ALU.add))
            link(v.tensor_tensor(Wn["L0_Wres"][:, :], Wn["L0_Wres"][:, :], ident[:, :], ALU.add))
            link(v.tensor_tensor(brow[:, 0, :], brow[:, 0, :], brow[:, 1, :], ALU.add))
            v.memset(stats[:, :, :, :], 0.0).then_inc(wt_ok, 1)
            dve.wait_ge(wt_ok, 1)
            ins = v.memset(l1_max, 0.0)
            link(ins)
            for i, k in enumerate(("L1_W1a", "L1_W1b", "L1_W2a", "L1_W2b")):
                v.tensor_reduce(l1_max[:, i:i + 1], WT[k][:, :], AX, ALU.max, apply_absolute_value=True)
            v.tensor_reduce(l1_max[:, 4:5], bcol[:, 1:3], AX, ALU.max, apply_absolute_value=True)
            link(v.tensor_reduce(l1_max[0:1, 5:6], brow[0:1, 2, :], AX, ALU.max, apply_absolute_value=True))
            link(v.tensor_reduce(flags[:, 3:4], l1_max, AX, ALU.max))
            link(v.tensor_scalar(flags[:, 3:4], flags[:, 3:4], L1_MAX, None, ALU.is_gt))

            dve.wait_ge(round_ok, 2)
            v.tensor_tensor(parts_even[:, 2], rest, parts_even[:, 1], ALU.subtract).then_inc(parts0_ok, 1)
            dve.wait_ge(parts0_ok, 1)

            for i in range(NC // CG):
                cs = slice(CG * i, CG * i + CG)
                dve.wait_ge(dblk_in[i], 16 * CG)
                link(v.tensor_tensor(cmp2[:, cs], dblk[:, cs], d_c[:, cs].to_broadcast([NP, CG, BLOCK]), ALU.is_lt))
                link(v.tensor_reduce(ptrf[:, cs], cmp2[:, cs], AX, ALU.add))
                link(v.scalar_tensor_tensor(ptrf[:, cs], blkf[:, cs], float(BLOCK), ptrf[:, cs], ALU.mult, ALU.add))
                link(v.tensor_scalar(ptrf[:, cs], ptrf[:, cs], float(EP - SLOTS), None, ALU.min))
                v.tensor_scalar(ptr3[:, cs], ptrf[:, cs], 3.0, None, ALU.mult)
                v.tensor_scalar(ptr8[:, cs], ptrf[:, cs], float(FE), None, ALU.mult).then_inc(ptr_ok, 1)

            last = SLOTS - 1
            v.memset(code_base[0:64], -2.0)
            v.memset(code_base[64:128], -1.0)
            for r_ in rec[:4]:
                v.memset(r_[:, NC, :], 0.0)
            for i in range(NC // CG):
                cs = slice(CG * i, CG * i + CG)
                dve.wait_ge(sd_in[i], 16 * CG)
                source, weight = sdw[:, cs, :, 0], sdw[:, cs, :, 2]
                hi, lo, w1, w2, cnt = (r_[:, cs, :] for r_ in rec)
                v.tensor_tensor(cnt, sdw[:, cs, :, 1], d_c[:, cs].to_broadcast([NP, CG, SLOTS]), ALU.is_equal)
                link(v.tensor_scalar(hi, source, 1.0 / NC, -0.5 + 0.5 / NC, ALU.mult, ALU.add))
                wm = w_slots[:, cs, :]
                v.tensor_tensor(wm, weight, cnt, ALU.mult)
                link(v.tensor_scalar(hi, hi, ROUND_MAGIC, -ROUND_MAGIC, ALU.add, ALU.add))
                v.tensor_copy(w1h[:, cs, :], wm)
                link(v.scalar_tensor_tensor(lo, hi, -float(NC), source, ALU.mult, ALU.add))
                v.tensor_reduce(w_max[:, i:i + 1], wm.rearrange("p c s -> p (c s)"), AX, ALU.max, apply_absolute_value=True)
                v.tensor_tensor(w2, wm, w1h[:, cs, :], ALU.subtract)
                v.scalar_tensor_tensor(lo, lo, 1.0, cnt, ALU.add, ALU.mult)
                v.tensor_copy(w1, w1h[:, cs, :]).then_inc(rec_ok, 1)
            dve.wait_ge(rec_ok, NC // CG)
            v.tensor_reduce(flags[0:NP, 1:2], cntR[:, 0:NC, last], AX, ALU.max)
            link(v.tensor_reduce(flags[0:NP, 2:3], w_max, AX, ALU.max))
            link(v.tensor_scalar(flags[0:NP, 2:3], flags[0:NP, 2:3], WEIGHT_MAX, None, ALU.is_gt))
            v.tensor_reduce(flags[:, 0:1], flags[:, :], AX, ALU.max).then_inc(flag_ok, 1)

            v.tensor_reduce(S8[:, :, 0], cntR[:, 0:NC, :], AX, ALU.add)
            link(v.tensor_reduce(S8[:, :, 1], w_slots, AX, ALU.add))

            def degrees():
                link(v.tensor_scalar(inv_n[:, :], S8[:, :, 0], 1.0, None, ALU.max))
                link(v.reciprocal(inv_n[:, :], inv_n[:, :]))
                v.tensor_scalar(degr[:, :], S8[:, :, 1], 1.0, None, ALU.add).then_inc(deg_ok, 1)

            degrees()

            dve.wait_ge(flag_ps, 1)
            v.tensor_copy(mode[:, :], ps[0:1, 6, 0:1]).then_inc(mode_ok, 1)

            def produce(q, u):
                b = u % 3
                cols = slice(u * TS, u * TS + TS)
                dve.wait_ge(sums_ok, BANKS * (STEPS * q + u + 1))
                v.tensor_tensor(hot_lo[b][:, 0], iota_lo,
                                lo_c[:, bass.ds(q, 1), cols].to_broadcast([128, 2 * NC, TS]),
                                ALU.is_equal).then_inc(eq_ok, 1)
                v.tensor_tensor(hot_hi[b], iota_hi,
                                hi_c[:, bass.ds(q, 1), cols].to_broadcast([128, 128, TS]), ALU.is_equal)
                dve.wait_ge(eq_ok, STEPS * q + u + 1)
                for k in range(2):
                    ins = v.tensor_tensor(hot_lo[b][:, 1 + k], hot_lo[b][:, 0],
                                          w_c[:, k, bass.ds(q, 1), cols].to_broadcast([128, 2 * NC, TS]), ALU.mult)
                ins.then_inc(hots_ok, 1)

            lns = [0]

            def layer_norm(dst, y, i, n):
                for c in range(n):
                    ins = v.bn_stats(stats[:, i, c, :], y[:, c, :])
                link(ins)
                for c in range(n):
                    ins = v.bn_aggr(mv[:, i, c, :], stats[:, i, c, :])
                ins.then_inc(var_ready, 1)
                lns[0] += 1
                dve.wait_ge(std_ready, lns[0])
                link(v.reciprocal(rstd[:, i, 0:n], std[:, i, 0:n]))
                for c in range(n):
                    ins = v.tensor_scalar(dst[:, c, :], y[:, c, :], mv[:, i, c, 0:1], rstd[:, i, c:c + 1],
                                          ALU.subtract, ALU.mult)
                return ins

            def split(r, g, n, src, general):
                if general:
                    if r and g == 0:
                        dve.wait_ge(g_stored, 16 * r)
                    v.tensor_copy(g_rows[:, GRP * g:GRP * g + n, :], src).then_inc(parts_ready, 1)
                    dve.wait_ge(parts_ready, GROUPS * r + g + 1)
                    return
                to = parts(r + 1)
                cs = slice(GRP * g, GRP * g + n)
                link(v.tensor_copy(to[:, 0, cs, :], src))
                if n_parts(r + 1) == 2:
                    v.tensor_tensor(to[:, 1, cs, :], src, to[:, 0, cs, :], ALU.subtract).then_inc(parts_ready, 1)
                else:
                    z = Z[g % 2][:, 0:n, :]
                    link(v.tensor_tensor(z, src, to[:, 0, cs, :], ALU.subtract))
                    link(v.tensor_copy(to[:, 1, cs, :], z))
                    v.tensor_tensor(to[:, 2, cs, :], z, to[:, 1, cs, :], ALU.subtract).then_inc(parts_ready, 1)

            def first_sum(q, general):
                r, g = divmod(q, GROUPS)
                n = chunks_of(g) * NP
                if r == 0 and not general:
                    dve.sem_inc(t1_ready, 1)
                    return
                t1 = T1[q % 2][:, 0:n]
                pa = g_sum[:, GCOL * g:GCOL * g + n] if general else ps[:, q % 2, 0:n]
                xt = XT[:, GCOL * g:GCOL * g + n]
                if not general:
                    dve.wait_ge(item_used, item_no[(r, g, 2 if layer_of(r) == 2 else 0)] + 1)
                if q >= 2:
                    dve.wait_ge(s2_done, q - 1)
                if r in (1, 2):
                    dve.wait_ge(rep_ok, g + 1)
                    dve.wait_ge(xt_ready, GROUPS * (r - 1) + g + 1)
                if layer_of(r) == 0:
                    v.tensor_tensor(t1, xt, pa, ALU.add).then_inc(t1_ready, 1)
                elif layer_of(r) == 1:
                    link(v.tensor_tensor(t1, pa, inv_deg[:, g, 0:n], ALU.mult))
                    v.tensor_tensor(t1, t1, xt, ALU.add).then_inc(t1_ready, 1)
                else:
                    v.tensor_copy(t1, pa).then_inc(t1_ready, 1)

            def finish(q, general):
                r, g = divmod(q, GROUPS)
                i, n = q % 2, chunks_of(g)
                cs = slice(GRP * g, GRP * g + n)
                y, z, xn = Y[i][:, 0:n, :], Z[i][:, 0:n, :], Xn[:, cs, :]
                pb = ps[0:NP, 2 + i, :].rearrange("p (c f) -> p c f", f=D)[:, 0:n, :]
                pc = ps[0:NP, 4 + i, :].rearrange("p (c f) -> p c f", f=D)[:, 0:n, :]
                scale = dinv[:, cs].unsqueeze(2).to_broadcast([NP, n, D])

                def bias(k):
                    return brow[:, k:k + 1, :].to_broadcast([NP, n, D])

                dve.wait_ge(s2_done, q + 1)
                if r == 0:
                    v.tensor_tensor(y, pc, bias(0), ALU.add).then_inc(s2_read, 1)
                    dve.wait_ge(s2_read, q + 1)
                    layer_norm(xn, y, i, n).then_inc(v_ready, 1)
                    dve.wait_ge(v_ready, q + 1)
                    split(r, g, n, xn, general)
                elif r == 1:
                    if g >= 2:
                        dve.wait_ge(s3_done, q - 1)
                    v.tensor_tensor(y, pc, bias(2), ALU.add).then_inc(s2_read, 1)
                    dve.wait_ge(s2_read, q + 1)
                    v.tensor_scalar(y, y, 0.0, None, ALU.max).then_inc(v_ready, 1)
                    dve.wait_ge(v_ready, q + 1)
                    split(r, g, n, y, general)
                elif r == 2:
                    dve.wait_ge(s3_done, q - 1)
                    v.tensor_tensor(y, pc, bias(3), ALU.add).then_inc(s2_read, 1)
                    dve.wait_ge(s2_read, q + 1)
                    link(v.scalar_tensor_tensor(y, y, 0.0, xn, ALU.max, ALU.add))
                    layer_norm(xn, y, i, n).then_inc(v_ready, 1)
                    dve.wait_ge(v_ready, q + 1)
                    v.tensor_copy(Cn[:, cs, :], xn)
                    link(v.tensor_tensor(z, xn, scale, ALU.mult))
                    split(r, g, n, z, general)
                elif layer_of(r) == 2:
                    cn = Cn[:, cs, :]
                    link(v.tensor_tensor(y, pb, scale, ALU.mult))
                    v.tensor_tensor(y, y, pc, ALU.add).then_inc(s2_read, 1)
                    dve.wait_ge(s2_read, q + 1)
                    v.tensor_tensor(y, y, bias(4), ALU.add).then_inc(pre_tanh, 1)
                    dve.wait_ge(tanh_ok, q - 3 * GROUPS + 1)
                    if r < 6:
                        v.scalar_tensor_tensor(cn, z, EPS_STEP, cn, ALU.mult, ALU.add).then_inc(v_ready, 1)
                        dve.wait_ge(v_ready, q + 1)
                        link(v.tensor_tensor(z, cn, scale, ALU.mult))
                        split(r, g, n, z, general)
                    else:
                        link(v.scalar_tensor_tensor(cn, z, EPS_STEP, cn, ALU.mult, ALU.add))
                        link(v.tensor_tensor(y, cn, xn, ALU.add))
                        link(layer_norm(xn, y, i, n))
                        split(r, g, n, xn, general)
                else:
                    v.scalar_tensor_tensor(y, pc, 0.0, xn, ALU.max, ALU.add).then_inc(s2_read, 1)
                    dve.wait_ge(s2_read, q + 1)
                    if g >= 2:
                        dve.wait_ge(y_out[g % 2], 16 * (g // 2))
                    layer_norm(z, y, i, n).then_inc(y_ready, 1)

            def attributes(c):
                buf = attrs[c % 3]
                link(v.tensor_scalar(slot_used, slot_no, S8[:, c, 0:1], None, ALU.is_lt))
                dve.wait_ge(attrs_in[c % 3], 16 * (c // 3 + 1))
                link(v.tensor_tensor(buf, buf, slot_used.unsqueeze(2).to_broadcast([NP, SLOTS, FE]), ALU.mult))
                v.tensor_reduce(S8[:, c, 2:FE], buf[:, :, 2:FE].rearrange("p s f -> p f s"), AX, ALU.add).then_inc(attrs_ok, 1)

            def fast():
                dve.wait_ge(iotas, 1)
                v.tensor_scalar(neg_ident, ident[:, :], -1.0, None, ALU.mult).then_inc(hots_ok, 1)
                dve.wait_ge(col_ok, 16)
                with dve.Fori(0, PAIRS) as q:
                    for u in range(STEPS):
                        produce(q, u)
                dve.wait_ge(sq_ok, 1)
                link(v.reciprocal(dinv[:, :], degr[:, :]))
                dve.wait_ge(xt0_ok, GROUPS)
                for q in range(ROUNDS * GROUPS):
                    first_sum(q, False)
                    finish(q, False)
                    if layer_of(q // GROUPS) == 2 and q - 3 * GROUPS < NC:
                        attributes(q - 3 * GROUPS)

            def general():
                dve.wait_ge(g_in, 32)
                dve.wait_ge(col_ok, 16)
                dve.wait_ge(g_consts, 1)
                link(v.tensor_copy(g_dst, g_pairs[:, :, 1]))

                def one_hots(a, m):
                    with dve.Fori(0, TILES // 2) as i:
                        for j in range(2):
                            tile = bass.ds(2 * i + j, 1)
                            dve.wait_ge(g_used, TILES * a + 2 * i + j + 1)
                            if a == 0:
                                v.tensor_copy(g_f8[j], g_feats[:, tile, :].rearrange("p a f -> p (a f)"))
                            v.tensor_scalar(g_hot[j], g_node, g_dst[:, tile], g_feats[:, tile, m],
                                            ALU.is_equal, ALU.mult).then_inc(g_hot_ok, 1)

                def take(a, n_part):
                    dve.wait_ge(g_used, TILES * (a + 1) + 2)
                    for g in range(GROUPS):
                        n = chunks_of(g) * NP
                        ins = v.tensor_copy(g_sum[0:n_part, GCOL * g:GCOL * g + n], ps[0:n_part, g, 0:n])
                    ins.then_inc(g_taken, 1)
                    dve.wait_ge(g_taken, a + 1)

                one_hots(0, 0)
                take(0, FE)
                dve.wait_ge(g_s8_ps, 1)
                link(v.tensor_copy(S8[:, :, :], ps[0:NP, 7, 0:NC * FE].rearrange("p (c f) -> p c f", f=FE)))
                dve.wait_ge(sq_ok, 1)
                degrees()
                dve.wait_ge(sq_ok, 2)
                link(v.reciprocal(dinv[:, :], degr[:, :]))
                dve.wait_ge(xt0_ok, GROUPS)
                for r in range(ROUNDS):
                    one_hots(r + 1, 1 if layer_of(r) == 2 else 0)
                    take(r + 1, 128)
                    for q in range(GROUPS * r, GROUPS * r + GROUPS):
                        first_sum(q, True)
                        finish(q, True)

            def count_again(path):
                def run():
                    at_branch = chain[0], lns[0]
                    path()
                    chain[0], lns[0] = at_branch
                return run

            by_mode(dve, count_again(fast), count_again(general))

        @block.scalar
        def _(act):
            s = nc.scalar
            for g in range(GROUPS):
                n = chunks_of(g) * NP
                act.wait_ge(xt_ps, g + 1)
                s.activation(XT[:, GCOL * g:GCOL * g + n], ps[:, 6 + g % 2, 0:n], ACT.Copy).then_inc(xt0_ok, 1)
            act.wait_ge(x_in, 16)
            s.activation(parts_even[:, 0], Xn[:, :, :], ACT.Copy).then_inc(round_ok, 1)
            act.wait_ge(rest0_ok, 1)
            s.activation(parts_even[:, 1], rest, ACT.Copy).then_inc(round_ok, 1)
            act.wait_ge(cols_zero, 1)
            for b in range(16):
                g, k = divmod(b, 4)
                n = min(4, PAIRS - 4 * g)
                act.wait_ge(col_ps, b + 1)
                src = ps[:, b % 4, 0:n * NP].rearrange("p (q t) -> p q t", t=NP)
                if k == 1:
                    ins = s.activation(lo_c[:, 4 * g:4 * g + n, :], src, ACT.Identity, bias=code_base, scale=2.0)
                else:
                    to = hi_c if k == 0 else w_c[:, k - 2]
                    ins = s.activation(to[:, 4 * g:4 * g + n, :], src, ACT.Copy)
                ins.then_inc(col_ok, 1)
            act.wait_ge(deg_ok, 1)
            s.activation(degr[:, :], degr[:, :], ACT.Sqrt).then_inc(sq_ok, 1)

            def relu_bias(q):
                r, g = divmod(q, GROUPS)
                n = chunks_of(g) * NP
                act.wait_ge(s1_done, q + 1)
                if q >= 2:
                    act.wait_ge(s2_done, q - 1)
                s.activation(T2[q % 2][:, 0:n], ps[:, 2 + q % 2, 0:n], ACT.Relu if r == 0 else ACT.Identity,
                             bias=bcol[:, r:r + 1]).then_inc(t2_ready, 1)

            def columns(q):
                r, g = divmod(q, GROUPS)
                n = chunks_of(g) * NP
                act.wait_ge(s3_done, q + 1)
                s.activation(XT[:, GCOL * g:GCOL * g + n], ps[:, 6 + q % 2, 0:n], ACT.Copy).then_inc(xt_ready, 1)

            def fast():
                def pair(q, first=False):
                    act.wait_ge(stg_free, q + 1)
                    act.wait_ge(agg0_done, q + 1)

                    def leave(i, low):
                        done = BANKS * STEPS * q + i + 1
                        act.wait_ge(rest_ok if low else sums_ok, done if low else done + AHEAD * BANKS)
                        src = ps[:, i % BANKS, 0:BT * 100].rearrange("p (t k n) -> p k n t", t=BT, k=2)[:, low:2]
                        dst = stg[:, bass.ds(q % 2, 1), 2 * low:2 + low, :, i * BT:i * BT + BT].rearrange("p a k n t -> p (a k) n t")
                        s.activation(dst, src, ACT.Copy).then_inc(bank_free if low else hi_out, 1)

                    for i in range(BANKS * STEPS):
                        leave(i, 0)
                        if i >= LAG:
                            leave(i - LAG, 1)
                    for i in range(BANKS * STEPS - LAG, BANKS * STEPS):
                        leave(i, 1)
                    if not first:
                        sum_out(q - 1, 2 * NP)

                def sum_out(q, n):
                    act.wait_ge(agg0_done, q + 3)
                    s.activation(sum0[:, bass.ds(q * (2 * NP), n)], ps[:, BANKS, 0:n], ACT.Copy).then_inc(sum0_out, 1)

                act.sem_inc(sum0_out, 1)
                pair(0, first=True)
                with act.Fori(1, PAIRS) as q:
                    pair(q)
                sum_out(PAIRS - 1, NP)

                after_build(False)

            def general():
                act.wait_ge(deg_ok, 2)
                s.activation(degr[:, :], degr[:, :], ACT.Sqrt).then_inc(sq_ok, 1)
                after_build(True)

            def after_build(general):
                def take_degrees(g):
                    n = chunks_of(g) * NP
                    act.wait_ge(rep_ps, g + 1)
                    s.activation(inv_deg[:, g, 0:n], ps[:, g % 2, 0:n], ACT.Copy).then_inc(rep_ok, 1)

                if general:
                    for g in range(GROUPS):
                        take_degrees(g)

                lns = [0]
                for q in range(ROUNDS * GROUPS):
                    r, g = divmod(q, GROUPS)
                    i, n = q % 2, chunks_of(g)
                    if r < 3:
                        relu_bias(q)
                    if r == 0 and not general:
                        take_degrees(g)
                    if r == 7:
                        act.wait_ge(s1_done, q + 1)
                        if g >= 2:
                            act.wait_ge(s2_done, q - 1)
                        s.activation(S8T[i][:, 0:n * NP], ps[0:FE, 2 + i, 0:n * NP], ACT.Copy).then_inc(t2_ready, 1)
                    if not general and 1 <= q and (q - 1) // GROUPS < 6:
                        columns(q - 1)
                    if layer_of(r) == 2:
                        act.wait_ge(pre_tanh, q - 3 * GROUPS + 1)
                        s.activation(Z[i][:, 0:n, :], Y[i][:, 0:n, :], ACT.Tanh).then_inc(tanh_ok, 1)
                    if r in (0, 2, 6, 7):
                        lns[0] += 1
                        act.wait_ge(var_ready, lns[0])
                        s.activation(std[:, i, 0:n], mv[:, i, 0:n, 1], ACT.Sqrt, bias=eps_col[0:NP, :]).then_inc(std_ready, 1)
                    if general and r < 6:
                        columns(q)

            by_mode(act, fast, general)

        @block.tensor
        def _(pe):
            t = nc.tensor
            for a in range(BT4):
                pe.wait_ge(before_ok, a + 1)
                for c in range(NC):
                    ins = t.matmul(ps[0:NP, 0, c:c + 1], before[:, a, c, :], blk_ones,
                                   start=(a == 0 and c == 0), stop=(a == BT4 - 1), skip_group_check=True)
            ins.then_inc(first_ps, 1)
            pe.wait_ge(consts, 2)
            pe.wait_ge(x_in, 16)
            for g in range(GROUPS):
                if g >= 2:
                    pe.wait_ge(xt0_ok, g - 1)
                for c in range(chunks_of(g)):
                    ins = t.transpose(ps[:, 6 + g % 2, c * NP:c * NP + NP], Xn[:, GRP * g + c, :], ident[0:NP, 0:NP])
                ins.then_inc(xt_ps, 1)
            pe.wait_ge(w_in, 16 * 21)
            for i, k in enumerate(WT):
                t.transpose(ps[:, 4 + i // 4, (i % 4) * D:(i % 4) * D + D], raw_w[:, i, :], ident[:, :]).then_inc(wt_ps, 1)
            for b in range(16):
                g, k = divmod(b, 4)
                if k == 0:
                    pe.wait_ge(rec_ok, -(-min(8 * g + 8, NC) // CG))
                if b >= 4:
                    pe.wait_ge(col_ok, b - 3)
                else:
                    pe.wait_ge(ptr_ok, 1)
                for j in range(min(4, PAIRS - 4 * g)):
                    q = 4 * g + j
                    ins = t.transpose(ps[:, b % 4, j * NP:j * NP + NP],
                                      rec[k][:, 2 * q:2 * q + 2, :].rearrange("p c s -> p (c s)"), ident[0:NP, 0:NP])
                ins.then_inc(col_ps, 1)

            def product1(q, general=False):
                r, g = divmod(q, GROUPS)
                n = chunks_of(g)
                bank = 2 + q % 2
                if q >= 2:
                    if r <= 2 or q - 2 < 3 * GROUPS:
                        pe.wait_ge(t2_ready, q - 1)
                    elif q - 2 < 7 * GROUPS:
                        pe.wait_ge(s2_read, q - 1)
                    else:
                        pe.wait_ge(t2_ready, q - 1 - 4 * GROUPS)
                if r < 3:
                    if r or general:
                        pe.wait_ge(t1_ready, q + 1)
                    lhs = (Wn["L0_W1"], WT["L1_W1a"], WT["L1_W2a"])[r]
                    rhs = T1[q % 2][:, 0:n * NP] if r or general else sum0[:, GCOL * g:GCOL * g + n * NP]
                    t.matmul(ps[:, bank, 0:n * NP], lhs[:, :], rhs, start=True, stop=True).then_inc(s1_done, 1)
                elif layer_of(r) == 2:
                    pe.wait_ge(t1_ready, q + 1)
                    for c in range(n):
                        ins = t.matmul(ps[0:NP, bank, c * D:c * D + D], T1[q % 2][:, c * NP:c * NP + NP],
                                       WT["L2_Wphi"][:, :], start=True, stop=True)
                    ins.then_inc(s1_done, 1)
                else:
                    if not general:
                        pe.wait_ge(attrs_ok, NC)
                    for c in range(n):
                        ins = t.transpose(ps[0:FE, bank, c * NP:c * NP + NP], S8[:, GRP * g + c, :], ident[0:NP, 0:NP])
                    ins.then_inc(s1_done, 1)

            def product2(q):
                r, g = divmod(q, GROUPS)
                n = chunks_of(g)
                if q >= 2:
                    pe.wait_ge(s2_read, q - 1)
                if r < 3:
                    pe.wait_ge(t2_ready, q + 1)
                if r == 7:
                    pe.wait_ge(t1_ready, q + 1)
                    pe.wait_ge(t2_ready, q + 1 - 4 * GROUPS)
                if layer_of(r) == 2:
                    pe.wait_ge(xt_ready, GROUPS * (r - 1) + g + 1)
                for c in range(n):
                    o = ps[0:NP, 4 + q % 2, c * D:c * D + D]
                    cols = slice(c * NP, c * NP + NP)
                    xt = XT[:, GCOL * g + c * NP:GCOL * g + c * NP + NP]
                    if r == 0:
                        terms = [(T2[q % 2][:, cols], Wn["L0_W2"]), (xt, Wn["L0_Wres"])]
                    elif layer_of(r) == 1:
                        terms = [(T2[q % 2][:, cols], WT["L1_W1b" if r == 1 else "L1_W2b"])]
                    elif layer_of(r) == 2:
                        terms = [(xt, WT["L2_W"])]
                    else:
                        terms = [(T1[q % 2][:, cols], Wn["L3_W"]), (S8T[q % 2][:, cols], W8)]
                    for i, (a, b) in enumerate(terms):
                        ins = t.matmul(o, a, b[:, :], start=(i == 0), stop=(i == len(terms) - 1))
                ins.then_inc(s2_done, 1)

            def transposes(q):
                r, g = divmod(q, GROUPS)
                pe.wait_ge(v_ready, q + 1)
                if q >= 2:
                    pe.wait_ge(xt_ready, q - 1)
                for c in range(chunks_of(g)):
                    k = GRP * g + c
                    src = Y[q % 2][:, c, :] if r == 1 else Cn[:, k, :] if layer_of(r) == 2 else Xn[:, k, :]
                    ins = t.transpose(ps[:, 6 + q % 2, c * NP:c * NP + NP], src, ident[0:NP, 0:NP])
                ins.then_inc(s3_done, 1)

            def need_parts(r, g, k_end):
                if g == 0:
                    if r == 0:
                        pe.wait_ge(parts0_ok, 1)
                    else:
                        pe.wait_ge(parts_ready, GROUPS * (r - 1) + -(-k_end // GRP))

            def aggregate(q):
                r, g = divmod(q, GROUPS)
                n = chunks_of(g) * NP
                o = ps[:, q % 2, 0:n]
                xs = parts(r)
                mine = [(r, g, m) for m in ((1, 2) if layer_of(r) == 2 else (0,))]
                if q >= GROUPS + 2:
                    pe.wait_ge(t1_ready, q - 1)
                else:
                    pe.wait_ge(rep_ok, q - 1)

                def step(it, k0, loop, first, final):
                    slot = ring[item_no[it] % RING][0:NP]
                    for kk in range(KCH):
                        k = k0 + kk
                        for j in range(n_parts(r)):
                            ks = bass.ds(k, 1) if loop else slice(k, k + 1)
                            rhs = (slot[:, :, ks, :] if n == GCOL else slot[:, 0:1, ks, 0:n])
                            if n == GCOL:
                                rhs = rhs.rearrange("p q a n -> p q (a n)")
                            else:
                                rhs = rhs.rearrange("p q a n -> p (q a n)")
                            lhs = xs[:, j, ks, :].rearrange("p a f -> p (a f)")
                            ins = t.matmul(o, lhs, rhs, start=(first and kk == 0 and j == 0),
                                           stop=(final and kk == KCH - 1 and j == n_parts(r) - 1))
                    return ins

                for a, it in enumerate(mine):
                    i = item_no[it]
                    pe.wait_ge(slot_in[i % RING], 16 * (i // RING + 1))
                    if a == 0:
                        need_parts(r, g, KCH)
                        step(it, 0, False, True, False)
                        if q >= 1:
                            product1(q - 1)
                        if q >= 2 and (q - 2) // GROUPS < 6:
                            transposes(q - 2)
                        need_parts(r, g, 2 * KCH)
                        step(it, KCH, False, False, False)
                        if q >= 1:
                            product2(q - 1)
                        need_parts(r, g, 4 * KCH)
                        k_from = 2 * KCH
                    else:
                        k_from = 0
                    with pe.Fori(k_from, 4 * KCH, KCH) as k0:
                        step(it, k0, True, False, False)
                    if a == 0:
                        need_parts(r, g, NC)
                    ins = step(it, 4 * KCH, False, False, a == len(mine) - 1)
                    ins.then_inc(item_used, 1)

            pe.wait_ge(flag_ok, 1)
            pe.wait_ge(xt0_ok, GROUPS)
            t.matmul(ps[0:1, 6, 0:1], flags[:, 0:1], one_col[:, :], start=True, stop=True).then_inc(flag_ps, 1)

            def spread_degrees(g):
                if g >= 2:
                    pe.wait_ge(rep_ok, g - 1)
                for c in range(chunks_of(g)):
                    k = GRP * g + c
                    ins = t.matmul(ps[:, g % 2, c * NP:c * NP + NP], inv_n[:, k:k + 1].to_broadcast([NP, 128]),
                                   ident[0:NP, 0:NP], start=True, stop=True)
                ins.then_inc(rep_ps, 1)

            def fast():
                pe.wait_ge(wt_ok, 1)
                pe.wait_ge(parts0_ok, 1)
                pe.sem_inc(sums_ok, AHEAD * BANKS)
                pe.sem_inc(bank_free, BANKS)
                pe.sem_inc(agg0_done, 2)

                def sum_counts(q, ks, n):
                    o = ps[:, BANKS, 0:n]
                    for k in ks:
                        if k == 0:
                            pe.wait_ge(sum0_out, q + 1)
                        for j in range(3):
                            rhs = stg[0:NP, bass.ds(q % 2, 1), 0, 2 * k:2 * k + n // NP, :].rearrange("p a n t -> p (a n t)")
                            t.matmul(o, parts_even[:, j, k, :], rhs, start=(k == 0 and j == 0), stop=False,
                                     skip_group_check=True)
                        if k == NC - 1:
                            t.matmul(o, ident[:, :], XT[:, bass.ds(q * (2 * NP), n)], start=False, stop=True,
                                     skip_group_check=True).then_inc(agg0_done, 1)

                def pair(q, first=False, last=False):
                    def take_high(i):
                        pe.wait_ge(hi_out, BANKS * STEPS * q + i + 1)
                        o = ps[:, i % BANKS, 0:BT * 100].rearrange("p (t k n) -> p k t n", t=BT, k=2)[:, 1]
                        high = stg[:, bass.ds(q % 2, 1), 1, :, i * BT:i * BT + BT].rearrange("p a n t -> p (a t) n")
                        t.matmul(o, neg_ident, high, start=False, stop=True, skip_group_check=True).then_inc(rest_ok, 1)

                    for u in range(STEPS):
                        b = u % 3
                        pe.wait_ge(hots_ok, STEPS * q + u + 2)
                        hot = hot_lo[b].rearrange("p k n t -> p (k n) t")
                        for bank in range(BANKS):
                            i = BANKS * u + bank
                            pe.wait_ge(bank_free, BANKS * STEPS * q + i + 1)
                            for e in range(BT):
                                o = e * 100
                                T = bank * BT + e
                                t.matmul(ps[:, bank, o:o + 100], hot_hi[b][:, :, T], hot[:, 0:100, T],
                                         start=(e == 0), stop=False, skip_group_check=True)
                                t.matmul(ps[:, bank, o + 50:o + 100], hot_hi[b][:, :, T], hot[:, 100:150, T],
                                         start=False, stop=False, skip_group_check=True)
                            weight_sums = ps[:, bank, 0:BT * 100].rearrange("p (t m) -> p t m", t=BT)[:, :, 50:100]
                            eye = neg_ident[:, i * BT:i * BT + BT].unsqueeze(2)
                            if last:
                                own = weight_sums[:, :, 4 * q:4 * q + 1]
                            else:
                                own = weight_sums[:, :, bass.ds(q * 4, 4)][:, :, 0:4:3]
                                eye = eye.to_broadcast([128, BT, 2])
                            t.matmul(own, neg_ident, eye, start=False, stop=True,
                                     skip_group_check=True).then_inc(sums_ok, 1)
                            if i >= LAG:
                                take_high(i - LAG)
                            if not first and u:
                                a, z = ((BANKS * (u - 1) + bank + d) * NC // (BANKS * (STEPS - 1)) for d in (0, 1))
                                sum_counts(q - 1, range(a, z), 2 * NP)
                    for i in range(BANKS * STEPS - LAG, BANKS * STEPS):
                        take_high(i)

                pair(0, first=True)
                with pe.Fori(1, PAIRS - 1) as q:
                    pair(q)
                pair(PAIRS - 1, last=True)
                sum_counts(PAIRS - 1, range(NC), NP)
                pe.wait_ge(bank_free, BANKS * BUILD + BANKS)
                pe.wait_ge(sum0_out, PAIRS + 1)
                product1(0)
                for g in range(1, GROUPS):
                    if g < GROUPS - 1:
                        product1(g)
                    spread_degrees(g - 1)
                    product2(g - 1)
                    if g >= 2:
                        transposes(g - 2)
                spread_degrees(GROUPS - 1)
                for q in range(GROUPS, ROUNDS * GROUPS):
                    aggregate(q)
                product1(ROUNDS * GROUPS - 1)
                product2(ROUNDS * GROUPS - 1)

            def general():
                pe.wait_ge(wt_ok, 1)
                pe.wait_ge(col_ok, 16)
                pe.wait_ge(g_consts, 1)
                pe.sem_inc(g_used, 2)

                def sums(a, lhs, n_part, own_rows):
                    for g in range(GROUPS):
                        n = chunks_of(g) * NP
                        t.matmul(ps[0:n_part, g, 0:n], g_zero[:, 0:n_part], g_node[:, GCOL * g:GCOL * g + n],
                                 start=True, stop=False, skip_group_check=True)
                    if own_rows:
                        for c in range(NC):
                            o = (c % GRP) * NP
                            t.matmul(ps[:, c // GRP, o:o + NP], g_rows[:, c, :], ident[0:NP, 0:NP],
                                     start=False, stop=False, skip_group_check=True)
                    with pe.Fori(0, TILES // 2) as i:
                        for j in range(2):
                            pe.wait_ge(g_hot_ok, TILES * a + 2 * i + j + 1)
                            if a:
                                pe.wait_ge(g_x_in[j], 8 * TILES * (a - 1) + 16 * i + 16)
                            for g in range(GROUPS):
                                n = chunks_of(g) * NP
                                ins = t.matmul(ps[0:n_part, g, 0:n], lhs[j], g_hot[j][:, GCOL * g:GCOL * g + n],
                                               start=False, stop=False, skip_group_check=True)
                            ins.then_inc(g_used, 1)

                pe.wait_ge(parts0_ok, 1)
                sums(0, g_f8, FE, False)
                pe.wait_ge(g_taken, 1)
                for c in range(NC):
                    ins = t.transpose(ps[0:NP, 7, c * FE:c * FE + FE], g_sum[0:FE, c * NP:c * NP + NP], ident[0:FE, 0:FE])
                ins.then_inc(g_s8_ps, 1)
                pe.wait_ge(deg_ok, 2)
                for g in range(GROUPS):
                    spread_degrees(g)
                pe.wait_ge(rep_ok, GROUPS)
                for r in range(ROUNDS):
                    if r:
                        pe.wait_ge(s2_read, GROUPS * r)
                        pe.wait_ge(xt_ready, GROUPS * min(r, 6))
                        pe.wait_ge(parts_ready, GROUPS * r)
                    sums(r + 1, g_x, 128, layer_of(r) == 2)
                    pe.wait_ge(g_taken, r + 2)
                    for q in range(GROUPS * r, GROUPS * r + GROUPS):
                        product1(q, general=True)
                        product2(q)
                        if r < 6:
                            transposes(q)

            by_mode(pe, fast, general)


_WEIGHTS = {
    "L0_W1": "L0_gnn_W1", "L0_b1": "L0_gnn_b1", "L0_W2": "L0_gnn_W2", "L0_b2": "L0_gnn_b2",
    "L0_Wres": "L0_gnn_Wres", "L0_bres": "L0_gnn_bres",
    "L1_W1a": "L1_gnn_W1a", "L1_b1a": "L1_gnn_b1a", "L1_W1b": "L1_gnn_W1b", "L1_b1b": "L1_gnn_b1b",
    "L1_W2a": "L1_gnn_W2a", "L1_b2a": "L1_gnn_b2a", "L1_W2b": "L1_gnn_W2b", "L1_b2b": "L1_gnn_b2b",
    "L2_W": "L2_gnn_W", "L2_bias": "L2_gnn_bias", "L2_Wphi": "L2_gnn_W_phi",
    "L3_W": "L3_gnn_W", "L3_b": "L3_gnn_b", "L3_We": "L3_gnn_We", "L3_be": "L3_gnn_be",
}


def kernel(**inputs):
    import numpy as np
    import concourse.bacc as bacc
    from concourse.bass_utils import run_bass_kernel_spmd

    pad = EP - EDGES
    src, dst = np.asarray(inputs["src"]), np.asarray(inputs["dst"])
    src = np.concatenate([src, np.zeros(pad, src.dtype)])
    dst = np.concatenate([dst, np.full(pad, NODES, dst.dtype)])
    attr, weight = np.asarray(inputs["edge_attr_6"]), np.asarray(inputs["edge_weight"])
    feats = np.concatenate([np.ones((EDGES, 1), weight.dtype), weight[:, None], attr], axis=1)
    feats = np.concatenate([feats, np.zeros((pad, FE), weight.dtype)])
    arrays = {
        "x": np.ascontiguousarray(inputs["x"]),
        "edge_pairs": np.ascontiguousarray(np.stack([src, dst], axis=1)),
        "edge_w": np.ascontiguousarray(feats[:, 1]),
        "dst_blocks": np.ascontiguousarray(dst.reshape(NBLK, BLOCK)),
        "edge_feats": np.ascontiguousarray(feats),
    }
    arrays.update({k: np.ascontiguousarray(inputs[name]) for k, name in _WEIGHTS.items()})
    nc = bacc.Bacc("TRN2", target_bir_lowering=False, num_devices=1)
    aps = {k: nc.dram_tensor("in_" + k, a.shape, mybir.dt.from_np(a.dtype), kind="ExternalInput").ap()
           for k, a in arrays.items()}
    out = nc.dram_tensor("out", (NODES, D), F32, kind="ExternalOutput").ap()
    build_program(nc, aps["x"], aps["edge_pairs"], aps["edge_w"], aps["dst_blocks"], aps["edge_feats"],
                  {k: aps[k] for k in _WEIGHTS}, out)
    r = run_bass_kernel_spmd(nc, [{"in_" + k: a for k, a in arrays.items()}], core_ids=[0])
    return r.results[0]["out"]
```
